# Optimizing a Trainium2 kernel written in Bass

```python
import numpy as np
import jax
import jax.numpy as jnp

def _softmax(x, axis=-1):
    return jax.nn.softmax(x, axis=axis)

def _gelu(x):
    return jax.nn.gelu(x, approximate=True)

def _silu(x):
    return jax.nn.silu(x)

def _sigmoid(x):
    return jax.nn.sigmoid(x)

def _layernorm(x, axis=-1, eps=1e-05):
    m = jnp.mean(x, axis=axis, keepdims=True)
    v = jnp.var(x, axis=axis, keepdims=True)
    return (x - m) / jnp.sqrt(v + eps)

def _scatter_add(tgt, idx, src, axis=0):
    return tgt.at[idx].add(src)

def _segment_sum(src, seg, n):
    return jax.ops.segment_sum(src, seg, n)
kernel_name = 'mk_prb_d1_jaxref_r8_ceba9a'

def setup_inputs(seed: int=0):
    np.random.seed(seed)
    _w = jnp.asarray

    def _L0_attn_setup():
        import jax, jax.numpy as jnp
        import numpy as np
        NUM_HEADS = 8
        CHUNK = 64

        def _retention(q, k, v):
            B, Hn, L, DK = q.shape
            DV = v.shape[-1]
            C = CHUNK
            N = L // C
            dt = q.dtype
            gamma = (1.0 - jnp.exp2(-5.0 - jnp.arange(Hn, dtype=jnp.float32))).astype(dt)
            q = q * DK ** (-0.5)
            idx = jnp.arange(C)
            diff = idx[:, None] - idx[None, :]
            D = jnp.where(diff >= 0, gamma[:, None, None] ** diff, 0.0).astype(dt)
            decay_q = (gamma[:, None] ** (idx[None, :] + 1)).astype(dt)
            decay_k = (gamma[:, None] ** (C - 1 - idx[None, :])).astype(dt)
            decay_s = (gamma ** C).astype(dt)

            def to_chunks(x):
                return jnp.moveaxis(x.reshape(B, Hn, N, C, -1), 2, 0)
            qs, ks, vs = map(to_chunks, (q, k, v))

            def step(S, x):
                qc, kc, vc = x
                attn = jnp.einsum('bhid,bhjd->bhij', qc, kc) * D
                o_intra = jnp.einsum('bhij,bhje->bhie', attn, vc)
                o_inter = jnp.einsum('bhid,bhde->bhie', qc * decay_q[None, :, :, None], S)
                S_new = decay_s[None, :, None, None] * S + jnp.einsum('bhjd,bhje->bhde', kc * decay_k[None, :, :, None], vc)
                return (S_new, o_intra + o_inter)
            S0 = jnp.zeros((B, Hn, DK, DV), dt)
            _, o = jax.lax.scan(step, S0, (qs, ks, vs))
            return jnp.moveaxis(o, 0, 2).reshape(B, Hn, L, DV)

        def _xavier(key, fan_in, fan_out, gain=2 ** (-2.5)):
            limit = gain * np.sqrt(6.0 / (fan_in + fan_out))
            return jax.random.uniform(key, (fan_in, fan_out), jnp.float32, -limit, limit)
        key = jax.random.key(seed)
        k0, k1, k2, k3, k4 = jax.random.split(key, 5)
        B, L, D = (2, 512, 128)
        return {'hidden_states': jax.random.normal(k0, (B, L, D), jnp.float32), 'rel_pos': jnp.zeros((1,), jnp.float32), 'Wq': _xavier(k1, D, D), 'Wk': _xavier(k2, D, D), 'Wv': _xavier(k3, D, D), 'Wo': _xavier(k4, D, D)}
    _L0_attn_in = _L0_attn_setup()

    def _L0_ffn_setup():
        import jax, jax.numpy as jnp
        import numpy as np

        def _bitlinear(x, w_latent):
            scale = jax.lax.stop_gradient(jnp.clip(jnp.mean(jnp.abs(w_latent), axis=1, keepdims=True), 1e-05, None))
            tern = jnp.clip(jnp.round(w_latent / scale), -1.0, 1.0)
            w = w_latent + jax.lax.stop_gradient(tern - w_latent)
            return x @ (w * scale).T
        key = jax.random.key(seed)
        ks = jax.random.split(key, 6)
        dim, hidden, rank = (128, 512, 16)
        B, S = (4, 512)
        x = jax.random.normal(ks[0], (B, S, dim), dtype=jnp.float32)
        w_fc = 0.02 * jax.random.normal(ks[1], (hidden, dim), dtype=jnp.float32)
        w_proj = 0.02 * jax.random.normal(ks[2], (dim, hidden), dtype=jnp.float32)
        u = 0.02 * jax.random.normal(ks[3], (hidden, rank), dtype=jnp.float32)
        v = 0.02 * jax.random.normal(ks[4], (rank, dim), dtype=jnp.float32)
        fast_b = jax.random.normal(ks[5], (rank, rank), dtype=jnp.float32)
        gate = jnp.float32(0.05)
        return {'x': x, 'fast_b': fast_b, 'w_fc': w_fc, 'w_proj': w_proj, 'u': u, 'v': v, 'gate': gate}
    _L0_ffn_in = _L0_ffn_setup()
    _d = {'L0_attn_hidden_states': _L0_attn_in['hidden_states'], 'L0_attn_rel_pos': _L0_attn_in['rel_pos'], 'L0_attn_Wq': _L0_attn_in['Wq'], 'L0_attn_Wk': _L0_attn_in['Wk'], 'L0_attn_Wv': _L0_attn_in['Wv'], 'L0_attn_Wo': _L0_attn_in['Wo'], 'L0_ffn_fast_b': _L0_ffn_in['fast_b'], 'L0_ffn_w_fc': _L0_ffn_in['w_fc'], 'L0_ffn_w_proj': _L0_ffn_in['w_proj'], 'L0_ffn_u': _L0_ffn_in['u'], 'L0_ffn_v': _L0_ffn_in['v'], 'L0_ffn_gate': _L0_ffn_in['gate']}
    _x0 = _d['L0_attn_hidden_states']
    _d['L0_attn_hidden_states'] = jax.random.normal(jax.random.fold_in(jax.random.key(seed), 1), (8, 512, 128), dtype=_x0.dtype)
    del _x0
    return _d

def reference(L0_attn_hidden_states, L0_attn_rel_pos, L0_attn_Wq, L0_attn_Wk, L0_attn_Wv, L0_attn_Wo, L0_ffn_fast_b, L0_ffn_w_fc, L0_ffn_w_proj, L0_ffn_u, L0_ffn_v, L0_ffn_gate):

    def _L0_attn_ref(hidden_states, rel_pos, Wq, Wk, Wv, Wo):
        import jax, jax.numpy as jnp
        import numpy as np
        NUM_HEADS = 8
        CHUNK = 64

        def _retention(q, k, v):
            B, Hn, L, DK = q.shape
            DV = v.shape[-1]
            C = CHUNK
            N = L // C
            dt = q.dtype
            gamma = (1.0 - jnp.exp2(-5.0 - jnp.arange(Hn, dtype=jnp.float32))).astype(dt)
            q = q * DK ** (-0.5)
            idx = jnp.arange(C)
            diff = idx[:, None] - idx[None, :]
            D = jnp.where(diff >= 0, gamma[:, None, None] ** diff, 0.0).astype(dt)
            decay_q = (gamma[:, None] ** (idx[None, :] + 1)).astype(dt)
            decay_k = (gamma[:, None] ** (C - 1 - idx[None, :])).astype(dt)
            decay_s = (gamma ** C).astype(dt)

            def to_chunks(x):
                return jnp.moveaxis(x.reshape(B, Hn, N, C, -1), 2, 0)
            qs, ks, vs = map(to_chunks, (q, k, v))

            def step(S, x):
                qc, kc, vc = x
                attn = jnp.einsum('bhid,bhjd->bhij', qc, kc) * D
                o_intra = jnp.einsum('bhij,bhje->bhie', attn, vc)
                o_inter = jnp.einsum('bhid,bhde->bhie', qc * decay_q[None, :, :, None], S)
                S_new = decay_s[None, :, None, None] * S + jnp.einsum('bhjd,bhje->bhde', kc * decay_k[None, :, :, None], vc)
                return (S_new, o_intra + o_inter)
            S0 = jnp.zeros((B, Hn, DK, DV), dt)
            _, o = jax.lax.scan(step, S0, (qs, ks, vs))
            return jnp.moveaxis(o, 0, 2).reshape(B, Hn, L, DV)

        def _xavier(key, fan_in, fan_out, gain=2 ** (-2.5)):
            limit = gain * np.sqrt(6.0 / (fan_in + fan_out))
            return jax.random.uniform(key, (fan_in, fan_out), jnp.float32, -limit, limit)
        B, L, Dm = hidden_states.shape
        Hd = Dm // NUM_HEADS
        q = (hidden_states @ Wq).reshape(B, L, NUM_HEADS, Hd).transpose(0, 2, 1, 3)
        k = (hidden_states @ Wk).reshape(B, L, NUM_HEADS, Hd).transpose(0, 2, 1, 3)
        v = (hidden_states @ Wv).reshape(B, L, NUM_HEADS, Hd).transpose(0, 2, 1, 3)
        o = _retention(q, k, v)
        o = o.transpose(0, 2, 1, 3).reshape(B, L, Dm)
        return o @ Wo

    def _L0_ffn_ref(x, fast_b, w_fc, w_proj, u, v, gate):
        import jax, jax.numpy as jnp
        import numpy as np

        def _bitlinear(x, w_latent):
            scale = jax.lax.stop_gradient(jnp.clip(jnp.mean(jnp.abs(w_latent), axis=1, keepdims=True), 1e-05, None))
            tern = jnp.clip(jnp.round(w_latent / scale), -1.0, 1.0)
            w = w_latent + jax.lax.stop_gradient(tern - w_latent)
            return x @ (w * scale).T
        h = _bitlinear(x, w_fc) + gate * (x @ v.T @ fast_b.T @ u.T)
        r = jnp.maximum(h, 0.0)
        return _bitlinear(r * r, w_proj)
    x = L0_attn_hidden_states
    xn = _layernorm(x, axis=-1)
    x = x + _L0_attn_ref(xn, L0_attn_rel_pos, L0_attn_Wq, L0_attn_Wk, L0_attn_Wv, L0_attn_Wo) + _L0_ffn_ref(xn, L0_ffn_fast_b, L0_ffn_w_fc, L0_ffn_w_proj, L0_ffn_u, L0_ffn_v, L0_ffn_gate)
    return x

_drawn_inputs = setup_inputs


def setup_inputs(seed=0):
    import zlib

    import numpy as np

    out = dict(_drawn_inputs(seed))
    spreads = {}
    factors = {'L0_attn_Wq': 2.826,
     'L0_attn_Wk': 2.746,
     'L0_attn_Wv': 2.822,
     'L0_attn_Wo': 2.774,
     'L0_ffn_fast_b': 8.0,
     'L0_ffn_w_fc': 5.22,
     'L0_ffn_w_proj': 4.135,
     'L0_ffn_u': 8.0,
     'L0_ffn_v': 8.0}
    for name, (base, spread) in spreads.items():
        noise = np.random.default_rng([zlib.crc32(name.encode()), seed]).standard_normal(out[name].shape)
        drawn = base * np.exp(spread * noise) if base else spread * noise
        out[name] = jnp.asarray(drawn.astype(out[name].dtype))
    for name, factor in factors.items():
        out[name] = (out[name] * factor).astype(out[name].dtype)
    return out
```

```python
from contextlib import ExitStack

import numpy as np

import concourse.bass as bass
from concourse import mybir

F32 = mybir.dt.float32
F32R = mybir.dt.float32r
ALU = mybir.AluOpType
ACT = mybir.ActivationFunctionType

P = 128
D = 128
H = 8
DK = D // H
SEQ = 512
NB = 8
TOK = NB * SEQ
CH = 64
NCH = SEQ // CH
NT = SEQ // P
FF = 512
NF = FF // P
RANK = 16
EPS = 1e-5
MIN_SCALE = 1e-5
HEADS_IN_GROUP = 2
NG = H // HEADS_IN_GROUP
GW = HEADS_IN_GROUP * DK

C_IDENT = 0
C_QTAB = C_IDENT + P
C_VTAB = C_QTAB + SEQ
C_BLOCK = C_VTAB + NT * H
C_CAUSAL = C_BLOCK + P
C_ALL = C_CAUSAL + CH


def constants():
    gamma = 1.0 - 2.0 ** (-5.0 - np.arange(H, dtype=np.float64))
    place = np.arange(SEQ)
    c = np.zeros((P, C_ALL), np.float64)
    c[:, C_IDENT:C_IDENT + P] = np.eye(P)
    head = np.arange(P) // DK
    c[:, C_QTAB:C_QTAB + SEQ] = gamma[head][:, None] ** (place + 1) * DK ** -0.5
    inverse = gamma[None, :] ** -(place[:, None] + 1.0)
    c[:, C_VTAB:C_VTAB + NT * H] = inverse.reshape(NT, P, H).transpose(1, 0, 2).reshape(P, NT * H)
    c[:, C_BLOCK:C_BLOCK + P] = head[:, None] == head[None, :]
    c[:, C_CAUSAL:C_CAUSAL + CH] = np.arange(CH)[None, :] >= (np.arange(P) % CH)[:, None]
    return c.astype(np.float32)


class Batch:

    def __init__(self, half, parity):
        self.half, self.parity = half, parity
        self.index = half * 2 + parity

    def next(self):
        return Batch(self.half, 1) if self.parity == 0 else Batch(self.half + 1, 0)

    def count(self, per_batch, k):
        return self.index * per_batch + k


def over_batches(engine, body):
    with engine.Fori(0, NB // 2 - 1) as half:
        for parity in range(2):
            body(Batch(half, parity), True)
    body(Batch(NB // 2 - 1, 0), True)
    body(Batch(NB // 2 - 1, 1), False)


def build(nc, x_tok, x_feat, wq, wk, wv, wo_t, fast_b_t, w_fc, w_proj, u_t, v_ffn, gate, const, out_feat):
    with ExitStack() as ctx:
        def sb(name, shape, dt=F32):
            return ctx.enter_context(nc.sbuf_tensor(name, shape, dt))

        def pb(name, shape):
            return ctx.enter_context(nc.psum_tensor(name, shape, F32))

        def sem(name):
            return ctx.enter_context(nc.semaphore(name))

        cst = sb("cst", [P, C_ALL])
        ident = cst[:, C_IDENT:C_IDENT + P]
        q_table = cst[:, C_QTAB:C_QTAB + SEQ]
        v_table = cst[:, C_VTAB:C_VTAB + NT * H].rearrange("p (t g s) -> p t g s", t=NT, s=HEADS_IN_GROUP)
        block_mask = cst[:, C_BLOCK:C_BLOCK + P]
        causal = cst[:, C_CAUSAL:C_CAUSAL + CH]
        wqkv = sb("wqkv", [P, 3, D])
        wqkv_hi = sb("wqkv_hi", [P, 3, D], F32R)
        wqkv_lo = sb("wqkv_lo", [P, 3, D], F32R)
        wo_in = sb("wo_in", [P, D])
        wo_scaled = sb("wo_scaled", [P, D])
        wo = sb("wo", [P, D])
        fc_in = sb("fc_in", [P, NF, D])
        fc_above = sb("fc_above", [P, NF, D])
        fc_below = sb("fc_below", [P, NF, D])
        fc_scaled = sb("fc_scaled", [P, NF, D])
        fc_t = sb("fc_t", [P, FF])
        w1 = sb("w1", [P, FF])
        w1_hi = sb("w1_hi", [P, FF], F32R)
        w1_lo = sb("w1_lo", [P, FF], F32R)
        proj_in = sb("proj_in", [P, FF])
        proj_below = sb("proj_below", [P, FF])
        proj_tern = sb("proj_tern", [P, FF])
        w2 = sb("w2", [P, NF, D], F32R)
        absolute = sb("absolute", [P, FF])
        fb_in = sb("fb_in", [RANK, RANK])
        u_in = sb("u_in", [RANK, FF])
        v_in = sb("v_in", [RANK, D])
        gate_in = sb("gate_in", [RANK, 1])
        fbv = sb("fbv", [RANK, D])
        sums = sb("sums", [P, NF + 1])
        scale = sb("scale", [P, NF + 1])
        half_scale = sb("half_scale", [P, NF + 1])
        neg_half = sb("neg_half", [P, NF + 1])
        inv_scale2 = sb("inv_scale2", [P, 1])

        x_in = [sb(f"x_in{p}", [P, NT, D]) for p in range(2)]
        resid = sb("resid", [P, TOK])
        stats = sb("stats", [P, NT, 6])
        mean_var = sb("mean_var", [P, NT, 2])
        var_eps = sb("var_eps", [P, NT])
        std = sb("std", [P, NT])
        rstd0 = sb("rstd0", [P, NT])
        newton = sb("newton", [P, NT])
        newton2 = sb("newton2", [P, NT])
        rstd = sb("rstd", [P, NT])
        xn = sb("xn", [P, NT, D])
        xn_hi = sb("xn_hi", [P, SEQ], F32R)
        xn_lo = sb("xn_lo", [P, SEQ], F32R)
        q_dec = [sb(f"q_dec{p}", [P, SEQ]) for p in range(2)]
        q_exp = sb("q_exp", [P, H, SEQ])
        k_feat = sb("k_feat", [P, SEQ])
        k_tok = [sb(f"k_tok{p}", [P, NT, D]) for p in range(2)]
        v_pad = [sb(f"v_pad{p}", [P, NT, NG, HEADS_IN_GROUP * GW]) for p in range(2)]
        scores = sb("scores", [P, NT, H, CH])
        state = [sb(f"state{p}", [P, D]) for p in range(2)]
        o_feat = sb("o_feat", [P, NT, 2, CH])
        relu = [sb(f"relu{p}", [P, SEQ]) for p in range(2)]
        square = sb("square", [P, NF, SEQ])
        sq_hi = sb("sq_hi", [P, NF, SEQ], F32R)
        sq_lo = sb("sq_lo", [P, NF, SEQ], F32R)

        ps_score = [pb(f"ps_score{p}", [P, H * CH]) for p in range(2)]
        ps_work = [pb(f"ps_work{p}", [P, SEQ]) for p in range(2)]
        ps_state = pb("ps_state", [P, SEQ])
        ps_o = [pb(f"ps_o{p}", [P, SEQ]) for p in range(2)]
        ps_y = pb("ps_y", [P, SEQ])

        consts_in, x_loaded = sem("consts_in"), [sem(f"x_loaded{p}") for p in range(2)]
        wqkv_in, fc_loaded, proj_loaded = sem("wqkv_in"), sem("fc_loaded"), sem("proj_loaded")
        rank_loaded, wo_loaded, resid_loaded = sem("rank_loaded"), sem("wo_loaded"), sem("resid_loaded")
        q_expanded, out_stored = sem("q_expanded"), sem("out_stored")
        zeroed, wqkv_rounded, wqkv_split = sem("zeroed"), sem("wqkv_rounded"), sem("wqkv_split")
        abs_summed, scale_step, fc_step = sem("abs_summed"), sem("scale_step"), sem("fc_step")
        fbv_done, fbv_gated, low_rank_done = sem("fbv_done"), sem("fbv_gated"), sem("low_rank_done")
        tern_ready, weights_turned = sem("tern_ready"), sem("weights_turned")
        weights_copied, w1_step, w1_split = sem("weights_copied"), sem("w1_step"), sem("w1_split")
        ln_step, var_ready, std_ready = sem("ln_step"), sem("var_ready"), sem("std_ready")
        rstd_ready, xn_ready = sem("rstd_ready"), sem("xn_ready")
        xt_done, xn_hi_ready, xn_lo_ready = sem("xt_done"), sem("xn_hi_ready"), sem("xn_lo_ready")
        q_done, k_done, vk_done = sem("q_done"), sem("k_done"), sem("vk_done")
        q_ready, k_ready, vk_ready = sem("q_ready"), sem("k_ready"), sem("vk_ready")
        scores_done, scores_ready = sem("scores_done"), sem("scores_ready")
        state_done, state_ready = sem("state_done"), sem("state_ready")
        o_done, o_ready = sem("o_done"), sem("o_ready")
        h_done, relu_ready, square_ready = sem("h_done"), sem("relu_ready"), sem("square_ready")
        hi_ready, lo_ready = sem("hi_ready"), sem("lo_ready")
        y_done, result_ready = sem("y_done"), sem("result_ready")

        x_rows = x_tok.rearrange("(n t p) d -> p n t d", t=NT, p=P)

        def v_slots(v):
            return v.rearrange("p t g (s e) -> p t g s e", e=DK)[:, :, :, 0:4:3, :]

        block = ctx.enter_context(nc.Block())

        @block.sync
        def _(sync):
            sync.dma_start(x_in[0][:], x_rows[:, 0]).then_inc(x_loaded[0], 16)
            sync.dma_start(cst[:], const).then_inc(consts_in, 16)
            sync.dma_start(x_in[1][:], x_rows[:, 1]).then_inc(x_loaded[1], 16)
            sync.dma_start(resid[:], x_feat).then_inc(resid_loaded, 16)

            def spread_q(b):
                sync.wait_ge(q_ready, b.count(1, 1))
                for h in range(H):
                    rows = slice(h * DK, (h + 1) * DK)
                    sync.dma_start(q_exp[rows, h, :], q_dec[b.parity][rows, :]).then_inc(q_expanded, 16)

            sync.wait_ge(zeroed, 1)
            spread_q(Batch(0, 0))

            def body(b, has_next, load_ahead):
                if load_ahead:
                    sync.wait_ge(xn_ready, b.count(1, 1))
                    src = x_tok[bass.ds((b.index + 2) * SEQ, SEQ), :].rearrange("(t p) d -> p t d", p=P)
                    sync.dma_start(x_in[b.parity][:], src).then_inc(x_loaded[b.parity], 16)
                if has_next:
                    spread_q(b.next())
                sync.wait_ge(result_ready, b.count(1, 1))
                cols = bass.ds(b.index * SEQ, SEQ)
                sync.dma_start(out_feat[:, cols], resid[:, cols]).then_inc(out_stored, 16)

            with sync.Fori(0, NB // 2 - 1) as half:
                for parity in range(2):
                    body(Batch(half, parity), True, True)
            body(Batch(NB // 2 - 1, 0), True, False)
            body(Batch(NB // 2 - 1, 1), False, False)
            sync.wait_ge(out_stored, 16 * NB)

        @block.gpsimd
        def _(pool):
            nc.gpsimd.memset(q_exp[:], 0.0).then_inc(zeroed, 1)
            for p in range(2):
                nc.gpsimd.memset(v_pad[p][:], 0.0).then_inc(zeroed, 1)

            def body(b, has_next):
                for f in range(NF):
                    pool.wait_ge(hi_ready, b.count(NF, f + 1))
                    nc.gpsimd.tensor_tensor(sq_lo[:, f, :], square[:, f, :], sq_hi[:, f, :].bitcast(F32),
                                            ALU.subtract).then_inc(lo_ready, 1)

            over_batches(pool, body)

        @block.scalar
        def _(act):
            for i, w in enumerate((wq, wk, wv)):
                act.dma_start(wqkv[:, i, :], w).then_inc(wqkv_in, 16)
            act.dma_start(fc_in[:], w_fc.rearrange("(t p) d -> p t d", p=P)).then_inc(fc_loaded, 16)
            act.dma_start(proj_in[:], w_proj).then_inc(proj_loaded, 16)
            for dst, src in ((fb_in, fast_b_t), (u_in, u_t), (v_in, v_ffn), (gate_in, gate)):
                act.dma_start(dst[:], src).then_inc(rank_loaded, 16)
            act.dma_start(wo_in[:], wo_t).then_inc(wo_loaded, 16)

            def root(b):
                act.wait_ge(var_ready, b.count(1, 1))
                nc.scalar.activation(std[:], var_eps[:], ACT.Sqrt).then_inc(std_ready, 1)

            def round_xn(b):
                act.wait_ge(xt_done, b.count(1, 1))
                nc.scalar.activation(xn_hi[:], ps_work[0][:], ACT.Copy).then_inc(xn_hi_ready, 1)

            def copy_k(b):
                act.wait_ge(k_done, b.count(1, 1))
                nc.scalar.activation(k_feat[:], ps_work[0][:], ACT.Copy).then_inc(k_ready, 1)

            root(Batch(0, 0))
            act.wait_ge(wqkv_in, 48)
            nc.scalar.activation(wqkv_hi[:], wqkv[:], ACT.Copy).then_inc(wqkv_rounded, 1)
            round_xn(Batch(0, 0))
            act.wait_ge(fc_loaded, 16)
            act.wait_ge(proj_loaded, 16)
            for t in range(NF):
                nc.scalar.activation(absolute[:, t * D:(t + 1) * D], fc_in[:, t, :], ACT.Abs,
                                     accum_out=sums[:, t:t + 1]).then_inc(abs_summed, 1)
            act.wait_ge(abs_summed, NF)
            nc.scalar.activation(absolute[:], proj_in[:], ACT.Abs,
                                 accum_out=sums[:, NF:NF + 1]).then_inc(abs_summed, 1)
            copy_k(Batch(0, 0))
            act.wait_ge(weights_turned, 3)
            nc.scalar.activation(fc_t[:], ps_score[0][:], ACT.Copy).then_inc(weights_copied, 1)
            nc.scalar.activation(w2[:], ps_o[0][:].rearrange("p (t d) -> p t d", d=D),
                                 ACT.Copy).then_inc(weights_copied, 1)
            nc.scalar.activation(wo[:], ps_o[1][:, 0:D], ACT.Copy).then_inc(weights_copied, 1)

            def body(b, has_next):
                if has_next:
                    root(b.next())
                for f in range(NF):
                    act.wait_ge(h_done, b.count(NF, f + 1))
                    nc.scalar.activation(relu[f % 2][:], ps_work[f % 2][:], ACT.Relu).then_inc(relu_ready, 1)
                    act.wait_ge(relu_ready, b.count(NF, f + 1))
                    nc.scalar.activation(square[:, f, :], relu[f % 2][:], ACT.Square).then_inc(square_ready, 1)
                if has_next:
                    round_xn(b.next())
                    copy_k(b.next())
                for side in range(2):
                    act.wait_ge(o_done, b.count(2, side + 1))
                    nc.scalar.activation(o_feat[:, :, side, :],
                                         ps_o[side][:, 0:NT * CH].rearrange("p (t c) -> p t c", c=CH),
                                         ACT.Copy).then_inc(o_ready, 1)

            over_batches(act, body)

        @block.vector
        def _(dve):
            LN_STEPS = 5

            def statistics(b):
                dve.wait_ge(x_loaded[b.parity], (b.half + 1) * 16)
                for t in range(NT):
                    ins = nc.vector.bn_stats(stats[:, t, :], x_in[b.parity][:, t, :])
                ins.then_inc(ln_step, 1)

            def variance(b):
                for t in range(NT):
                    ins = nc.vector.bn_aggr(mean_var[:, t, :], stats[:, t, :])
                ins.then_inc(ln_step, 1)
                dve.wait_ge(ln_step, b.count(LN_STEPS, 2))
                nc.vector.tensor_scalar(var_eps[:], mean_var[:, :, 1], EPS, None, ALU.add).then_inc(var_ready, 1)

            def normalise(b):
                dve.wait_ge(std_ready, b.count(1, 1))
                nc.vector.reciprocal(rstd0[:], std[:]).then_inc(ln_step, 1)
                dve.wait_ge(ln_step, b.count(LN_STEPS, 3))
                nc.vector.tensor_tensor(newton[:], rstd0[:], var_eps[:], ALU.mult).then_inc(ln_step, 1)
                dve.wait_ge(ln_step, b.count(LN_STEPS, 4))
                nc.vector.scalar_tensor_tensor(out=newton2[:], in0=newton[:], scalar=-0.5, in1=rstd0[:],
                                               op0=ALU.mult, op1=ALU.mult).then_inc(ln_step, 1)
                dve.wait_ge(ln_step, b.count(LN_STEPS, 5))
                nc.vector.scalar_tensor_tensor(out=rstd[:], in0=newton2[:], scalar=1.5, in1=rstd0[:],
                                               op0=ALU.add, op1=ALU.mult).then_inc(rstd_ready, 1)
                dve.wait_ge(rstd_ready, b.count(1, 1))
                for t in range(NT):
                    ins = nc.vector.tensor_scalar(xn[:, t, :], x_in[b.parity][:, t, :], mean_var[:, t, 0:1],
                                                  rstd[:, t:t + 1], ALU.subtract, ALU.mult)
                ins.then_inc(xn_ready, 1)

            def low_xn(b):
                dve.wait_ge(xn_hi_ready, b.count(1, 1))
                nc.vector.tensor_tensor(xn_lo[:], ps_work[0][:], xn_hi[:].bitcast(F32),
                                        ALU.subtract).then_inc(xn_lo_ready, 1)

            def decay_q(b):
                dve.wait_ge(q_done, b.count(1, 1))
                nc.vector.tensor_tensor(q_dec[b.parity][:], ps_work[1][:], q_table,
                                        ALU.mult).then_inc(q_ready, 1)

            def take_vk(b, side):
                dve.wait_ge(vk_done, b.count(2, side + 1))
                bank = ps_work[1 - side][:].rearrange("p (t w) -> p t w", t=2)
                tiles = slice(2 * side, 2 * side + 2)
                for t in range(2):
                    tile = 2 * side + t
                    nc.vector.tensor_tensor(
                        v_slots(v_pad[b.parity][:])[:, tile],
                        bank[:, t, 0:D].rearrange("p (g s e) -> p g s e", s=HEADS_IN_GROUP, e=DK),
                        v_table[:, tile].unsqueeze(3).broadcast_to([P, NG, HEADS_IN_GROUP, DK]), ALU.mult)
                nc.vector.tensor_copy(k_tok[b.parity][:, tiles, :], bank[:, :, D:2 * D]).then_inc(vk_ready, 1)

            def mask_scores(b, pair):
                dve.wait_ge(scores_done, b.count(NT, pair + 1))
                nc.vector.tensor_tensor(
                    scores[:, pair], ps_score[pair % 2][:].rearrange("p (h i) -> p h i", h=H),
                    causal.unsqueeze(1).broadcast_to([P, H, CH]), ALU.mult).then_inc(scores_ready, 1)

            def take_state(b, c):
                dve.wait_ge(state_done, b.count(NCH - 1, c))
                nc.vector.tensor_tensor(state[c % 2][:], ps_state[:, 0:D], block_mask,
                                        ALU.mult).then_inc(state_ready, 1)

            def high_square(b, f):
                dve.wait_ge(square_ready, b.count(NF, f + 1))
                nc.vector.tensor_copy(sq_hi[:, f, :], square[:, f, :]).then_inc(hi_ready, 1)

            def finish(b):
                dve.wait_ge(y_done, b.count(1, 1))
                cols = bass.ds(b.index * SEQ, SEQ)
                nc.vector.scalar_tensor_tensor(out=resid[:, cols], in0=ps_y[:], scalar=scale[:, NF:NF + 1],
                                               in1=resid[:, cols], op0=ALU.mult,
                                               op1=ALU.add).then_inc(result_ready, 1)

            first = Batch(0, 0)
            statistics(first)
            dve.wait_ge(ln_step, 1)
            variance(first)
            normalise(first)
            dve.wait_ge(wqkv_rounded, 1)
            nc.vector.tensor_tensor(wqkv_lo[:], wqkv[:], wqkv_hi[:].bitcast(F32),
                                    ALU.subtract).then_inc(wqkv_split, 1)
            low_xn(first)
            dve.wait_ge(consts_in, 16)
            decay_q(first)
            dve.wait_ge(zeroed, 3)
            dve.wait_ge(fbv_done, 1)
            dve.wait_ge(rank_loaded, 64)
            nc.vector.tensor_scalar(fbv[:], ps_y[0:RANK, 0:D], gate_in[:], None, ALU.mult).then_inc(fbv_gated, 1)
            for side in range(2):
                take_vk(first, side)
            dve.wait_ge(abs_summed, NF + 1)
            nc.vector.tensor_scalar(scale[:, 0:NF], sums[:, 0:NF], 1.0 / D, MIN_SCALE, ALU.mult, ALU.max)
            nc.vector.tensor_scalar(scale[:, NF:], sums[:, NF:], 1.0 / FF, MIN_SCALE, ALU.mult,
                                    ALU.max).then_inc(scale_step, 1)
            dve.wait_ge(scale_step, 1)
            nc.vector.tensor_scalar(half_scale[:], scale[:], 0.5, None, ALU.mult)
            nc.vector.tensor_scalar(neg_half[:], scale[:], -0.5, None, ALU.mult)
            nc.vector.reciprocal(inv_scale2[:], scale[:, NF:]).then_inc(scale_step, 1)
            dve.wait_ge(scale_step, 2)
            for t in range(NF):
                nc.vector.tensor_scalar(fc_above[:, t, :], fc_in[:, t, :], half_scale[:, t:t + 1],
                                        scale[:, t:t + 1], ALU.is_gt, ALU.mult)
                nc.vector.tensor_scalar(fc_below[:, t, :], fc_in[:, t, :], neg_half[:, t:t + 1],
                                        scale[:, t:t + 1], ALU.is_lt, ALU.mult)
            nc.vector.tensor_scalar(proj_below[:], proj_in[:], neg_half[:, NF:], None,
                                    ALU.is_lt).then_inc(fc_step, 1)
            dve.wait_ge(fc_step, 1)
            nc.vector.tensor_tensor(fc_scaled[:], fc_above[:], fc_below[:], ALU.subtract).then_inc(tern_ready, 1)
            nc.vector.scalar_tensor_tensor(out=proj_tern[:], in0=proj_in[:], scalar=half_scale[:, NF:],
                                           in1=proj_below[:], op0=ALU.is_gt,
                                           op1=ALU.subtract).then_inc(tern_ready, 1)
            dve.wait_ge(wo_loaded, 16)
            nc.vector.tensor_scalar(wo_scaled[:], wo_in[:], inv_scale2[:], None, ALU.mult).then_inc(tern_ready, 1)
            dve.wait_ge(weights_copied, 1)
            dve.wait_ge(low_rank_done, 1)
            nc.vector.tensor_tensor(w1[:], ps_score[1][:], fc_t[:], ALU.add).then_inc(w1_step, 1)
            dve.wait_ge(w1_step, 1)
            nc.vector.tensor_copy(w1_hi[:], w1[:]).then_inc(w1_step, 1)
            dve.wait_ge(w1_step, 2)
            nc.vector.tensor_tensor(w1_lo[:], w1[:], w1_hi[:].bitcast(F32), ALU.subtract).then_inc(w1_split, 1)
            dve.wait_ge(resid_loaded, 16)

            def body(b, has_next):
                nxt = b.next()
                if has_next:
                    statistics(nxt)
                    dve.wait_ge(ln_step, nxt.count(LN_STEPS, 1))
                mask_scores(b, 0)
                if has_next:
                    variance(nxt)
                    normalise(nxt)
                mask_scores(b, 1)
                take_state(b, 1)
                high_square(b, 0)
                mask_scores(b, 2)
                high_square(b, 1)
                mask_scores(b, 3)
                high_square(b, 2)
                take_state(b, 2)
                high_square(b, 3)
                if has_next:
                    low_xn(nxt)
                take_state(b, 3)
                if has_next:
                    decay_q(nxt)
                take_state(b, 4)
                take_state(b, 5)
                if has_next:
                    take_vk(nxt, 0)
                take_state(b, 6)
                if has_next:
                    take_vk(nxt, 1)
                take_state(b, 7)
                finish(b)

            over_batches(dve, body)

        @block.tensor
        def _(pe):
            mm = nc.tensor.matmul

            def turn_xn(b, after=None):
                pe.wait_ge(xn_ready, b.count(1, 1))
                if after is not None:
                    pe.wait_ge(relu_ready, after.count(NF, 3))
                for t in range(NT):
                    ins = nc.tensor.transpose(ps_work[0][:, t * P:(t + 1) * P], xn[:, t, :], ident)
                ins.then_inc(xt_done, 1)

            def three_terms(out, w_hi, w_lo, x_hi, x_lo):
                mm(out, w_hi, x_hi, start=True, stop=False)
                mm(out, w_hi, x_lo, start=False, stop=False)
                return mm(out, w_lo, x_hi, start=False, stop=True)

            def project_q(b, after=None):
                pe.wait_ge(xn_hi_ready, b.count(1, 1))
                pe.wait_ge(xn_lo_ready, b.count(1, 1))
                if after is not None:
                    pe.wait_ge(relu_ready, after.count(NF, 4))
                three_terms(ps_work[1][:], wqkv_hi[:, 0, :], wqkv_lo[:, 0, :], xn_hi[:], xn_lo[:]).then_inc(q_done, 1)

            def project_k(b):
                three_terms(ps_work[0][:], wqkv_hi[:, 1, :], wqkv_lo[:, 1, :], xn_hi[:], xn_lo[:]).then_inc(k_done, 1)

            def project_vk(b, side):
                pe.wait_ge(q_ready if side == 0 else k_ready, b.count(1, 1))
                for t in range(2):
                    toks = slice((2 * side + t) * P, (2 * side + t + 1) * P)
                    out = ps_work[1 - side][:, t * 2 * D:(t + 1) * 2 * D]
                    vk_hi, vk_lo = wqkv_hi[:, 2:0:-1, :], wqkv_lo[:, 2:0:-1, :]
                    mm(out, xn_hi[:, toks], vk_hi, start=True, stop=False)
                    mm(out, xn_hi[:, toks], vk_lo, start=False, stop=False)
                    ins = mm(out, xn_lo[:, toks], vk_hi, start=False, stop=True)
                ins.then_inc(vk_done, 1)

            def score(b, pair):
                if pair == 0:
                    pe.wait_ge(k_ready, b.count(1, 1))
                    pe.wait_ge(q_expanded, b.count(16 * H, 16 * H))
                if pair >= 2:
                    pe.wait_ge(scores_ready, b.count(NT, pair - 1))
                for side in range(2):
                    toks = slice((2 * pair + side) * CH, (2 * pair + side + 1) * CH)
                    ins = mm(ps_score[pair % 2][side * CH:(side + 1) * CH, :], k_feat[:, toks],
                             q_exp[:, :, toks], start=True, stop=True)
                ins.then_inc(scores_done, 1)

            def hidden(b, f):
                if f == 0:
                    pe.wait_ge(vk_ready, b.count(2, 2))
                if f >= 2:
                    pe.wait_ge(relu_ready, b.count(NF, f - 1))
                cols = slice(f * P, (f + 1) * P)
                three_terms(ps_work[f % 2][:], w1_hi[:, cols], w1_lo[:, cols], xn_hi[:], xn_lo[:]).then_inc(h_done, 1)

            def chunk(b, c):
                pair, side = c // 2, c % 2
                rows = slice(side * CH, (side + 1) * CH)
                cols = slice(pair * CH, (pair + 1) * CH)
                if c == 0:
                    pe.wait_ge(vk_ready, b.count(2, 2))
                if side == 0:
                    pe.wait_ge(scores_ready, b.count(NT, pair + 1))
                if c > 0:
                    pe.wait_ge(state_ready, b.count(NCH - 1, c))
                if c < NCH - 1:
                    mm(ps_state[:, 0:D], k_tok[b.parity][rows, pair, :],
                       v_slots(v_pad[b.parity][:])[rows, pair], start=(c == 0), stop=True,
                       skip_group_check=True).then_inc(state_done, 1)
                if c > 0:
                    mm(ps_o[side][:, cols], state[c % 2][:],
                       q_dec[b.parity][:, c * CH:(c + 1) * CH], start=True, stop=False)
                for s in range(HEADS_IN_GROUP):
                    for g in range(NG):
                        ins = mm(ps_o[side][g * GW:(g + 1) * GW, cols],
                                 v_pad[b.parity][rows, pair, g, s * GW:(s + 1) * GW],
                                 scores[rows, pair, g * HEADS_IN_GROUP + s, :],
                                 start=(c == 0 and s == 0), stop=(s == HEADS_IN_GROUP - 1))
                if c >= NCH - 2:
                    ins.then_inc(o_done, 1)

            def result(b):
                for f in range(NF):
                    pe.wait_ge(hi_ready, b.count(NF, f + 1))
                    mm(ps_y[:], w2[:, f, :], sq_hi[:, f, :], start=(f == 0), stop=False)
                    pe.wait_ge(lo_ready, b.count(NF, f + 1))
                    mm(ps_y[:], w2[:, f, :], sq_lo[:, f, :], start=False, stop=False)
                pe.wait_ge(o_ready, b.count(2, 2))
                mm(ps_y[:], wo[:], o_feat[:].rearrange("p t s c -> p (t s c)"), start=False,
                   stop=True).then_inc(y_done, 1)

            first = Batch(0, 0)
            pe.wait_ge(consts_in, 16)
            turn_xn(first)
            pe.wait_ge(wqkv_split, 1)
            project_q(first)
            project_k(first)
            pe.wait_ge(rank_loaded, 64)
            mm(ps_y[0:RANK, 0:D], fb_in[:], v_in[:], start=True, stop=True).then_inc(fbv_done, 1)
            for side in range(2):
                project_vk(first, side)
            pe.wait_ge(fbv_gated, 1)
            mm(ps_score[1][:], fbv[:], u_in[:], start=True, stop=True).then_inc(low_rank_done, 1)
            pe.wait_ge(tern_ready, 1)
            for t in range(NF):
                ins = nc.tensor.transpose(ps_score[0][:, t * P:(t + 1) * P], fc_scaled[:, t, :], ident)
            ins.then_inc(weights_turned, 1)
            pe.wait_ge(tern_ready, 2)
            for t in range(NF):
                ins = nc.tensor.transpose(ps_o[0][:, t * P:(t + 1) * P], proj_tern[:, t * P:(t + 1) * P], ident)
            ins.then_inc(weights_turned, 1)
            pe.wait_ge(tern_ready, 3)
            nc.tensor.transpose(ps_o[1][:, 0:D], wo_scaled[:], ident).then_inc(weights_turned, 1)
            pe.wait_ge(weights_copied, 3)
            pe.wait_ge(w1_split, 1)

            def body(b, has_next):
                nxt = b.next()
                score(b, 0)
                hidden(b, 0)
                score(b, 1)
                hidden(b, 1)
                chunk(b, 0)
                score(b, 2)
                hidden(b, 2)
                score(b, 3)
                hidden(b, 3)
                chunk(b, 1)
                if has_next:
                    turn_xn(nxt, b)
                chunk(b, 2)
                if has_next:
                    project_q(nxt, b)
                chunk(b, 3)
                if has_next:
                    project_k(nxt)
                chunk(b, 4)
                if has_next:
                    project_vk(nxt, 0)
                chunk(b, 5)
                if has_next:
                    project_vk(nxt, 1)
                chunk(b, 6)
                chunk(b, 7)
                result(b)

            over_batches(pe, body)


def kernel(L0_attn_hidden_states, L0_attn_rel_pos, L0_attn_Wq, L0_attn_Wk, L0_attn_Wv, L0_attn_Wo,
           L0_ffn_fast_b, L0_ffn_w_fc, L0_ffn_w_proj, L0_ffn_u, L0_ffn_v, L0_ffn_gate):
    import concourse.bacc as bacc
    from concourse.bass_utils import run_bass_kernel_spmd

    x = np.asarray(L0_attn_hidden_states).reshape(TOK, D)
    arrays = {
        "x_tok": x,
        "x_feat": x.T,
        "wq": np.asarray(L0_attn_Wq),
        "wk": np.asarray(L0_attn_Wk),
        "wv": np.asarray(L0_attn_Wv),
        "wo_t": np.asarray(L0_attn_Wo).T,
        "fast_b_t": np.asarray(L0_ffn_fast_b).T,
        "w_fc": np.asarray(L0_ffn_w_fc),
        "w_proj": np.asarray(L0_ffn_w_proj),
        "u_t": np.asarray(L0_ffn_u).T,
        "v_ffn": np.asarray(L0_ffn_v),
        "gate": np.broadcast_to(np.asarray(L0_ffn_gate).reshape(1, 1), (RANK, 1)),
        "const": constants(),
    }
    arrays = {name: np.ascontiguousarray(a) for name, a in arrays.items()}
    nc = bacc.Bacc("TRN2", target_bir_lowering=False, num_devices=1)
    args = [nc.dram_tensor(name, a.shape, mybir.dt.from_np(a.dtype), kind="ExternalInput").ap()
            for name, a in arrays.items()]
    out = nc.dram_tensor("out_feat", (D, TOK), F32, kind="ExternalOutput").ap()
    build(nc, *args, out)
    r = run_bass_kernel_spmd(nc, [arrays], core_ids=[0])
    got = np.asarray(r.results[0]["out_feat"])
    return np.ascontiguousarray(got.T).reshape(NB, SEQ, D)
```

```python
from contextlib import ExitStack

import numpy as np

import concourse.bass as bass
from concourse import mybir

F32 = mybir.dt.float32
F32R = mybir.dt.float32r
ALU = mybir.AluOpType
ACT = mybir.ActivationFunctionType

P = 128
D = 128
H = 8
DK = D // H
SEQ = 512
NB = 8
TOK = NB * SEQ
CH = 64
NCH = SEQ // CH
NT = SEQ // P
FF = 512
NF = FF // P
RANK = 16
EPS = 1e-5
MIN_SCALE = 1e-5
HEADS_IN_GROUP = 2
NG = H // HEADS_IN_GROUP
GW = HEADS_IN_GROUP * DK
DVE_HEADS = 4

C_IDENT = 0
C_QTAB = C_IDENT + P
C_VTAB = C_QTAB + SEQ
C_BLOCK = C_VTAB + NT * H
C_CAUSAL = C_BLOCK + P
C_ROWS = C_CAUSAL + CH
C_ALL = C_ROWS + H


def constants():
    gamma = 1.0 - 2.0 ** (-5.0 - np.arange(H, dtype=np.float64))
    place = np.arange(SEQ)
    c = np.zeros((P, C_ALL), np.float64)
    c[:, C_IDENT:C_IDENT + P] = np.eye(P)
    head = np.arange(P) // DK
    c[:, C_QTAB:C_QTAB + SEQ] = gamma[head][:, None] ** (place + 1) * DK ** -0.5
    inverse = gamma[None, :] ** -(place[:, None] + 1.0)
    c[:, C_VTAB:C_VTAB + NT * H] = inverse.reshape(NT, P, H).transpose(1, 0, 2).reshape(P, NT * H)
    c[:, C_BLOCK:C_BLOCK + P] = head[:, None] == head[None, :]
    c[:, C_CAUSAL:C_CAUSAL + CH] = np.arange(CH)[None, :] >= (np.arange(P) % CH)[:, None]
    c[:, C_ROWS:C_ROWS + H] = head[:, None] == np.arange(H)[None, :]
    return c.astype(np.float32)


class Batch:

    def __init__(self, half, parity):
        self.half, self.parity = half, parity
        self.index = half * 2 + parity

    def next(self):
        return Batch(self.half, 1) if self.parity == 0 else Batch(self.half + 1, 0)

    def count(self, per_batch, k):
        return self.index * per_batch + k


def over_batches(engine, body):
    with engine.Fori(0, NB // 2 - 1) as half:
        for parity in range(2):
            body(Batch(half, parity), 2)
    body(Batch(NB // 2 - 1, 0), 1)
    body(Batch(NB // 2 - 1, 1), 0)


def build(nc, x_tok, x_feat, qkv_weights, ffn_weights, rank_weights, const, out_feat):
    with ExitStack() as ctx:
        def sb(name, shape, dt=F32):
            return ctx.enter_context(nc.sbuf_tensor(name, shape, dt))

        def pb(name, shape):
            return ctx.enter_context(nc.psum_tensor(name, shape, F32))

        def sem(name):
            return ctx.enter_context(nc.semaphore(name))

        cst = sb("cst", [P, C_ALL])
        ident = cst[:, C_IDENT:C_IDENT + P]
        q_table = cst[:, C_QTAB:C_QTAB + SEQ]
        v_table = cst[:, C_VTAB:C_VTAB + NT * H].rearrange("p (t g s) -> p t g s", t=NT, s=HEADS_IN_GROUP)
        block_mask = cst[:, C_BLOCK:C_BLOCK + P]
        causal = cst[:, C_CAUSAL:C_CAUSAL + CH]
        head_rows = cst[:, C_ROWS:C_ROWS + H]
        wqkv = sb("wqkv", [P, 3, D])
        wqkv_hi = sb("wqkv_hi", [P, 3, D], F32R)
        wqkv_lo = sb("wqkv_lo", [P, 3, D], F32R)
        ffn_in = sb("ffn_in", [P, NF * D + FF + D])
        fc_in = ffn_in[:, 0:NF * D].rearrange("p (t d) -> p t d", d=D)
        proj_in = ffn_in[:, NF * D:NF * D + FF]
        wo_in = ffn_in[:, NF * D + FF:]
        wo_scaled = sb("wo_scaled", [P, D])
        wo = sb("wo", [P, D])
        fc_above = sb("fc_above", [P, NF, D])
        fc_below = sb("fc_below", [P, NF, D])
        fc_scaled = sb("fc_scaled", [P, NF, D])
        fc_t = sb("fc_t", [P, FF])
        w1 = sb("w1", [P, FF])
        w1_hi = sb("w1_hi", [P, FF], F32R)
        w1_lo = sb("w1_lo", [P, FF], F32R)
        proj_below = sb("proj_below", [P, FF])
        proj_tern = sb("proj_tern", [P, FF])
        w2 = sb("w2", [P, NF, D], F32R)
        absolute = sb("absolute", [P, FF])
        rank_in = sb("rank_in", [RANK, RANK + FF + D + 1])
        fb_in = rank_in[:, 0:RANK]
        u_in = rank_in[:, RANK:RANK + FF]
        v_in = rank_in[:, RANK + FF:RANK + FF + D]
        gate_in = rank_in[:, RANK + FF + D:]
        fbv = sb("fbv", [RANK, D])
        sums = sb("sums", [P, NF + 1])
        scale = sb("scale", [P, NF + 1])
        half_scale = sb("half_scale", [P, NF + 1])
        neg_half = sb("neg_half", [P, NF + 1])
        inv_scale2 = sb("inv_scale2", [P, 1])

        x_in = [sb(f"x_in{p}", [P, NT, D]) for p in range(2)]
        resid = sb("resid", [P, TOK])
        stats = sb("stats", [P, NT, 6])
        mean_var = sb("mean_var", [P, NT, 2])
        var_eps = sb("var_eps", [P, NT])
        std = sb("std", [P, NT])
        rstd0 = sb("rstd0", [P, NT])
        newton = sb("newton", [P, NT])
        newton2 = sb("newton2", [P, NT])
        rstd = sb("rstd", [P, NT])
        xn = sb("xn", [P, NT, D])
        xn_hi = sb("xn_hi", [P, SEQ], F32R)
        xn_lo = sb("xn_lo", [P, SEQ], F32R)
        q_dec = [sb(f"q_dec{p}", [P, SEQ]) for p in range(2)]
        q_exp = [sb(f"q_exp{p}", [P, H, SEQ]) for p in range(2)]
        k_feat = [sb(f"k_feat{p}", [P, SEQ]) for p in range(2)]
        k_tok = [sb(f"k_tok{p}", [P, NT, D]) for p in range(2)]
        v_pad = [sb(f"v_pad{p}", [P, NT, NG, HEADS_IN_GROUP * GW]) for p in range(2)]
        scores = sb("scores", [P, NT, H, CH])
        state = [sb(f"state{p}", [P, D]) for p in range(2)]
        o_feat = sb("o_feat", [P, NT, 2, CH])
        relu = [sb(f"relu{p}", [P, SEQ]) for p in range(2)]
        square = sb("square", [P, NF, SEQ])
        sq_hi = sb("sq_hi", [P, NF, SEQ], F32R)
        sq_lo = sb("sq_lo", [P, NF, SEQ], F32R)

        ps_score = [pb(f"ps_score{p}", [P, H * CH]) for p in range(2)]
        ps_work = [pb(f"ps_work{p}", [P, SEQ]) for p in range(2)]
        ps_state = pb("ps_state", [P, SEQ])
        ps_o = [pb(f"ps_o{p}", [P, SEQ]) for p in range(2)]
        ps_y = pb("ps_y", [P, SEQ])

        consts_in, x_loaded = sem("consts_in"), [sem(f"x_loaded{p}") for p in range(2)]
        wqkv_in, ffn_loaded, rank_loaded = sem("wqkv_in"), sem("ffn_loaded"), sem("rank_loaded")
        resid_loaded, out_stored = sem("resid_loaded"), sem("out_stored")
        zeroed, wqkv_rounded, wqkv_split = sem("zeroed"), sem("wqkv_rounded"), sem("wqkv_split")
        abs_summed, scale_step, fc_step = sem("abs_summed"), sem("scale_step"), sem("fc_step")
        fbv_done, fbv_gated, low_rank_done = sem("fbv_done"), sem("fbv_gated"), sem("low_rank_done")
        tern_ready, weights_turned = sem("tern_ready"), sem("weights_turned")
        weights_copied, w1_step, w1_split = sem("weights_copied"), sem("w1_step"), sem("w1_split")
        ln_step, var_ready, std_ready = sem("ln_step"), sem("var_ready"), sem("std_ready")
        rstd_ready, xn_ready = sem("rstd_ready"), sem("xn_ready")
        xt_done, xn_hi_ready, xn_lo_ready = sem("xt_done"), sem("xn_hi_ready"), sem("xn_lo_ready")
        q_done, k_done, vk_done = sem("q_done"), sem("k_done"), sem("vk_done")
        q_ready, k_ready, vk_ready = sem("q_ready"), sem("k_ready"), sem("vk_ready")
        q_heads_dve, q_heads_act = sem("q_heads_dve"), sem("q_heads_act")
        scores_done, scores_ready = sem("scores_done"), sem("scores_ready")
        state_done, state_ready = sem("state_done"), sem("state_ready")
        o_done, o_ready = sem("o_done"), sem("o_ready")
        h_done, relu_ready, square_ready = sem("h_done"), sem("relu_ready"), sem("square_ready")
        hi_ready, lo_ready = sem("hi_ready"), sem("lo_ready")
        y_done, result_ready = sem("y_done"), sem("result_ready")

        x_rows = x_tok.rearrange("(n t p) d -> p n t d", t=NT, p=P)

        def v_slots(v):
            return v.rearrange("p t g (s e) -> p t g s e", e=DK)[:, :, :, 0:4:3, :]

        block = ctx.enter_context(nc.Block())

        @block.sync
        def _(sync):
            sync.dma_start(x_in[0][:], x_rows[:, 0]).then_inc(x_loaded[0], 16)
            sync.dma_start(ffn_in[:], ffn_weights).then_inc(ffn_loaded, 16)
            sync.dma_start(cst[:], const).then_inc(consts_in, 16)
            sync.dma_start(x_in[1][:], x_rows[:, 1]).then_inc(x_loaded[1], 16)
            sync.dma_start(rank_in[:], rank_weights).then_inc(rank_loaded, 16)
            sync.dma_start(resid[:], x_feat).then_inc(resid_loaded, 16)

            def load_x(b, into):
                sync.wait_ge(xn_ready, b.index - 1)
                src = x_tok[bass.ds(b.index * SEQ, SEQ), :].rearrange("(t p) d -> p t d", p=P)
                sync.dma_start(x_in[into][:], src).then_inc(x_loaded[into], 16)

            def store(b):
                sync.wait_ge(result_ready, b.count(1, 1))
                cols = bass.ds(b.index * SEQ, SEQ)
                sync.dma_start(out_feat[:, cols], resid[:, cols]).then_inc(out_stored, 16)

            for parity in range(2):
                load_x(Batch(1, parity), parity)
            with sync.Fori(0, NB // 2 - 2) as half:
                for parity in range(2):
                    load_x(Batch(half + 2, parity), parity)
                    store(Batch(half, parity))
            with sync.Fori(NB // 2 - 2, NB // 2) as half:
                for parity in range(2):
                    store(Batch(half, parity))
            sync.wait_ge(out_stored, 16 * NB)

        @block.gpsimd
        def _(pool):
            for p in range(2):
                nc.gpsimd.memset(v_pad[p][:], 0.0).then_inc(zeroed, 1)

            def body(b, later):
                for f in range(NF):
                    pool.wait_ge(hi_ready, b.count(NF, f + 1))
                    nc.gpsimd.tensor_tensor(sq_lo[:, f, :], square[:, f, :], sq_hi[:, f, :].bitcast(F32),
                                            ALU.subtract).then_inc(lo_ready, 1)

            over_batches(pool, body)

        @block.scalar
        def _(act):
            act.dma_start(wqkv[:], qkv_weights).then_inc(wqkv_in, 16)

            def root(b):
                act.wait_ge(var_ready, b.count(1, 1))
                nc.scalar.activation(std[:], var_eps[:], ACT.Sqrt).then_inc(std_ready, 1)

            def round_xn(b):
                act.wait_ge(xt_done, b.count(1, 1))
                nc.scalar.activation(xn_hi[:], ps_work[0][:], ACT.Copy).then_inc(xn_hi_ready, 1)

            def copy_k(b):
                act.wait_ge(k_done, b.count(1, 1))
                nc.scalar.activation(k_feat[b.parity][:], ps_work[0][:], ACT.Copy).then_inc(k_ready, 1)

            def spread_q(b):
                act.wait_ge(q_ready, b.count(1, 1))
                for h in range(DVE_HEADS, H):
                    ins = nc.scalar.activation(q_exp[b.parity][:, h, :], q_dec[b.parity][:], ACT.Copy,
                                               scale=head_rows[:, h:h + 1])
                ins.then_inc(q_heads_act, 1)

            first = Batch(0, 0)
            root(first)
            act.wait_ge(ffn_loaded, 16)
            for t in range(NF):
                nc.scalar.activation(absolute[:, t * D:(t + 1) * D], fc_in[:, t, :], ACT.Abs,
                                     accum_out=sums[:, t:t + 1]).then_inc(abs_summed, 1)
            act.wait_ge(wqkv_in, 16)
            nc.scalar.activation(wqkv_hi[:], wqkv[:], ACT.Copy).then_inc(wqkv_rounded, 1)
            round_xn(first)
            act.wait_ge(abs_summed, NF)
            nc.scalar.activation(absolute[:], proj_in, ACT.Abs,
                                 accum_out=sums[:, NF:NF + 1]).then_inc(abs_summed, 1)
            act.wait_ge(consts_in, 16)
            spread_q(first)
            copy_k(first)
            root(first.next())
            act.wait_ge(weights_turned, 1)
            nc.scalar.activation(fc_t[:], ps_o[0][:], ACT.Copy).then_inc(weights_copied, 1)
            act.wait_ge(weights_turned, 2)
            nc.scalar.activation(w2[:], ps_state[:].rearrange("p (t d) -> p t d", d=D),
                                 ACT.Copy).then_inc(weights_copied, 1)
            act.wait_ge(weights_turned, 3)
            nc.scalar.activation(wo[:], ps_y[:, 0:D], ACT.Copy).then_inc(weights_copied, 1)

            def take_relu(b, f):
                act.wait_ge(h_done, b.count(NF, f + 1))
                nc.scalar.activation(relu[f % 2][:], ps_work[f % 2][:], ACT.Relu).then_inc(relu_ready, 1)

            def take_square(b, f):
                act.wait_ge(relu_ready, b.count(NF, f + 1))
                nc.scalar.activation(square[:, f, :], relu[f % 2][:], ACT.Square).then_inc(square_ready, 1)

            def body(b, later):
                nxt, ahead = b.next(), b.next().next()
                take_relu(b, 0)
                take_square(b, 0)
                if later > 1:
                    root(ahead)
                take_relu(b, 1)
                take_square(b, 1)
                take_relu(b, 2)
                take_square(b, 2)
                take_relu(b, 3)
                if later > 0:
                    round_xn(nxt)
                take_square(b, 3)
                if later > 0:
                    spread_q(nxt)
                    copy_k(nxt)
                for side in range(2):
                    act.wait_ge(o_done, b.count(2, side + 1))
                    nc.scalar.activation(o_feat[:, :, side, :],
                                         ps_o[side][:, 0:NT * CH].rearrange("p (t c) -> p t c", c=CH),
                                         ACT.Copy).then_inc(o_ready, 1)

            over_batches(act, body)

        @block.vector
        def _(dve):
            LN_STEPS = 5

            def statistics(b):
                dve.wait_ge(x_loaded[b.parity], (b.half + 1) * 16)
                for t in range(NT):
                    ins = nc.vector.bn_stats(stats[:, t, :], x_in[b.parity][:, t, :])
                ins.then_inc(ln_step, 1)

            def variance(b):
                for t in range(NT):
                    ins = nc.vector.bn_aggr(mean_var[:, t, :], stats[:, t, :])
                ins.then_inc(ln_step, 1)
                dve.wait_ge(ln_step, b.count(LN_STEPS, 2))
                nc.vector.tensor_scalar(var_eps[:], mean_var[:, :, 1], EPS, None, ALU.add).then_inc(var_ready, 1)

            def inverse_root(b, step):
                if step == 0:
                    dve.wait_ge(std_ready, b.count(1, 1))
                    nc.vector.reciprocal(rstd0[:], std[:]).then_inc(ln_step, 1)
                elif step == 1:
                    dve.wait_ge(ln_step, b.count(LN_STEPS, 3))
                    nc.vector.tensor_tensor(newton[:], rstd0[:], var_eps[:], ALU.mult).then_inc(ln_step, 1)
                elif step == 2:
                    dve.wait_ge(ln_step, b.count(LN_STEPS, 4))
                    nc.vector.scalar_tensor_tensor(out=newton2[:], in0=newton[:], scalar=-0.5, in1=rstd0[:],
                                                   op0=ALU.mult, op1=ALU.mult).then_inc(ln_step, 1)
                else:
                    dve.wait_ge(ln_step, b.count(LN_STEPS, 5))
                    nc.vector.scalar_tensor_tensor(out=rstd[:], in0=newton2[:], scalar=1.5, in1=rstd0[:],
                                                   op0=ALU.add, op1=ALU.mult).then_inc(rstd_ready, 1)

            def normalise(b):
                dve.wait_ge(rstd_ready, b.count(1, 1))
                for t in range(NT):
                    ins = nc.vector.tensor_scalar(xn[:, t, :], x_in[b.parity][:, t, :], mean_var[:, t, 0:1],
                                                  rstd[:, t:t + 1], ALU.subtract, ALU.mult)
                ins.then_inc(xn_ready, 1)

            def low_xn(b):
                dve.wait_ge(xn_hi_ready, b.count(1, 1))
                nc.vector.tensor_tensor(xn_lo[:], ps_work[0][:], xn_hi[:].bitcast(F32),
                                        ALU.subtract).then_inc(xn_lo_ready, 1)

            def decay_q(b):
                dve.wait_ge(q_done, b.count(1, 1))
                nc.vector.tensor_tensor(q_dec[b.parity][:], ps_work[1][:], q_table,
                                        ALU.mult).then_inc(q_ready, 1)

            def spread_q(b, part):
                dve.wait_ge(q_ready, b.count(1, 1))
                for h in range(part * DVE_HEADS // 2, (part + 1) * DVE_HEADS // 2):
                    ins = nc.vector.tensor_scalar(q_exp[b.parity][:, h, :], q_dec[b.parity][:],
                                                  head_rows[:, h:h + 1], None, ALU.mult)
                ins.then_inc(q_heads_dve, 1)

            def take_vk(b, side):
                dve.wait_ge(vk_done, b.count(2, side + 1))
                bank = ps_work[1 - side][:].rearrange("p (t w) -> p t w", t=2)
                tiles = slice(2 * side, 2 * side + 2)
                for t in range(2):
                    tile = 2 * side + t
                    nc.vector.tensor_tensor(
                        v_slots(v_pad[b.parity][:])[:, tile],
                        bank[:, t, 0:D].rearrange("p (g s e) -> p g s e", s=HEADS_IN_GROUP, e=DK),
                        v_table[:, tile].unsqueeze(3).broadcast_to([P, NG, HEADS_IN_GROUP, DK]), ALU.mult)
                nc.vector.tensor_copy(k_tok[b.parity][:, tiles, :], bank[:, :, D:2 * D]).then_inc(vk_ready, 1)

            def mask_scores(b, pair):
                dve.wait_ge(scores_done, b.count(NT, pair + 1))
                nc.vector.tensor_tensor(
                    scores[:, pair], ps_score[pair % 2][:].rearrange("p (h i) -> p h i", h=H),
                    causal.unsqueeze(1).broadcast_to([P, H, CH]), ALU.mult).then_inc(scores_ready, 1)

            def take_state(b, c):
                dve.wait_ge(state_done, b.count(NCH - 1, c))
                nc.vector.tensor_tensor(state[c % 2][:], ps_state[:, 0:D], block_mask,
                                        ALU.mult).then_inc(state_ready, 1)

            def high_square(b, f):
                dve.wait_ge(square_ready, b.count(NF, f + 1))
                nc.vector.tensor_copy(sq_hi[:, f, :], square[:, f, :]).then_inc(hi_ready, 1)

            def finish(b):
                dve.wait_ge(y_done, b.count(1, 1))
                cols = bass.ds(b.index * SEQ, SEQ)
                nc.vector.scalar_tensor_tensor(out=resid[:, cols], in0=ps_y[:], scalar=scale[:, NF:NF + 1],
                                               in1=resid[:, cols], op0=ALU.mult,
                                               op1=ALU.add).then_inc(result_ready, 1)

            first = Batch(0, 0)
            statistics(first)
            dve.wait_ge(ln_step, 1)
            variance(first)
            for step in range(4):
                inverse_root(first, step)
            normalise(first)
            dve.wait_ge(abs_summed, NF)
            nc.vector.tensor_scalar(scale[:, 0:NF], sums[:, 0:NF], 1.0 / D, MIN_SCALE, ALU.mult,
                                    ALU.max).then_inc(scale_step, 1)
            dve.wait_ge(scale_step, 1)
            nc.vector.tensor_scalar(half_scale[:, 0:NF], scale[:, 0:NF], 0.5, None, ALU.mult)
            nc.vector.tensor_scalar(neg_half[:, 0:NF], scale[:, 0:NF], -0.5, None, ALU.mult).then_inc(scale_step, 1)
            dve.wait_ge(wqkv_rounded, 1)
            nc.vector.tensor_tensor(wqkv_lo[:], wqkv[:], wqkv_hi[:].bitcast(F32),
                                    ALU.subtract).then_inc(wqkv_split, 1)
            dve.wait_ge(scale_step, 2)

            def ternary_fc(t):
                nc.vector.tensor_scalar(fc_above[:, t, :], fc_in[:, t, :], half_scale[:, t:t + 1],
                                        scale[:, t:t + 1], ALU.is_gt, ALU.mult)
                return nc.vector.tensor_scalar(fc_below[:, t, :], fc_in[:, t, :], neg_half[:, t:t + 1],
                                               scale[:, t:t + 1], ALU.is_lt, ALU.mult)

            ternary_fc(0)
            low_xn(first)
            statistics(first.next())
            ternary_fc(1)
            ternary_fc(2)
            ternary_fc(3).then_inc(fc_step, 1)
            dve.wait_ge(ln_step, first.next().count(LN_STEPS, 1))
            variance(first.next())
            dve.wait_ge(consts_in, 16)
            decay_q(first)
            dve.wait_ge(fc_step, 1)
            nc.vector.tensor_tensor(fc_scaled[:], fc_above[:], fc_below[:], ALU.subtract).then_inc(tern_ready, 1)
            spread_q(first, 0)
            spread_q(first, 1)
            dve.wait_ge(fbv_done, 1)
            nc.vector.tensor_scalar(fbv[:], ps_y[0:RANK, 0:D], gate_in, None, ALU.mult).then_inc(fbv_gated, 1)
            dve.wait_ge(zeroed, 2)
            take_vk(first, 0)
            dve.wait_ge(weights_copied, 1)
            dve.wait_ge(low_rank_done, 1)
            nc.vector.tensor_tensor(w1[:], ps_o[1][:], fc_t[:], ALU.add).then_inc(w1_step, 1)
            take_vk(first, 1)
            dve.wait_ge(w1_step, 1)
            nc.vector.tensor_copy(w1_hi[:], w1[:]).then_inc(w1_step, 1)
            dve.wait_ge(w1_step, 2)
            nc.vector.tensor_tensor(w1_lo[:], w1[:], w1_hi[:].bitcast(F32), ALU.subtract).then_inc(w1_split, 1)
            dve.wait_ge(abs_summed, NF + 1)
            nc.vector.tensor_scalar(scale[:, NF:], sums[:, NF:], 1.0 / FF, MIN_SCALE, ALU.mult,
                                    ALU.max).then_inc(scale_step, 1)
            dve.wait_ge(scale_step, 3)
            nc.vector.tensor_scalar(half_scale[:, NF:], scale[:, NF:], 0.5, None, ALU.mult)
            nc.vector.tensor_scalar(neg_half[:, NF:], scale[:, NF:], -0.5, None, ALU.mult)
            nc.vector.reciprocal(inv_scale2[:], scale[:, NF:]).then_inc(scale_step, 1)
            dve.wait_ge(scale_step, 4)
            nc.vector.tensor_scalar(wo_scaled[:], wo_in, inv_scale2[:], None, ALU.mult)
            nc.vector.tensor_scalar(proj_below[:], proj_in, neg_half[:, NF:], None, ALU.is_lt).then_inc(fc_step, 1)
            dve.wait_ge(fc_step, 2)
            nc.vector.scalar_tensor_tensor(out=proj_tern[:], in0=proj_in, scalar=half_scale[:, NF:],
                                           in1=proj_below[:], op0=ALU.is_gt,
                                           op1=ALU.subtract).then_inc(tern_ready, 1)
            for step in range(4):
                inverse_root(first.next(), step)
            normalise(first.next())
            dve.wait_ge(resid_loaded, 16)

            def body(b, later):
                nxt, ahead = b.next(), b.next().next()

                if later > 1:
                    statistics(ahead)
                    dve.wait_ge(ln_step, ahead.count(LN_STEPS, 1))
                mask_scores(b, 0)
                if later > 1:
                    variance(ahead)
                mask_scores(b, 1)
                high_square(b, 0)
                take_state(b, 1)
                if later > 1:
                    inverse_root(ahead, 0)
                high_square(b, 1)
                if later > 1:
                    inverse_root(ahead, 1)
                take_state(b, 2)
                if later > 1:
                    inverse_root(ahead, 2)
                high_square(b, 2)
                if later > 1:
                    inverse_root(ahead, 3)
                take_state(b, 3)
                if later > 0:
                    low_xn(nxt)
                high_square(b, 3)
                mask_scores(b, 2)
                if later > 0:
                    decay_q(nxt)
                take_state(b, 4)
                if later > 0:
                    spread_q(nxt, 0)
                take_state(b, 5)
                if later > 0:
                    spread_q(nxt, 1)
                mask_scores(b, 3)
                if later > 0:
                    take_vk(nxt, 0)
                take_state(b, 6)
                if later > 0:
                    take_vk(nxt, 1)
                take_state(b, 7)
                if later > 1:
                    normalise(ahead)
                finish(b)

            over_batches(dve, body)

        @block.tensor
        def _(pe):
            mm = nc.tensor.matmul

            def turn_xn(b, after=None):
                pe.wait_ge(xn_ready, b.count(1, 1))
                if after is not None:
                    pe.wait_ge(relu_ready, after.count(NF, 3))
                for t in range(NT):
                    ins = nc.tensor.transpose(ps_work[0][:, t * P:(t + 1) * P], xn[:, t, :], ident)
                ins.then_inc(xt_done, 1)

            def three_terms(out, w_hi, w_lo, x_hi, x_lo):
                mm(out, w_hi, x_hi, start=True, stop=False)
                mm(out, w_hi, x_lo, start=False, stop=False)
                return mm(out, w_lo, x_hi, start=False, stop=True)

            def project_q(b, after=None):
                pe.wait_ge(xn_hi_ready, b.count(1, 1))
                pe.wait_ge(xn_lo_ready, b.count(1, 1))
                if after is not None:
                    pe.wait_ge(relu_ready, after.count(NF, 4))
                three_terms(ps_work[1][:], wqkv_hi[:, 0, :], wqkv_lo[:, 0, :], xn_hi[:], xn_lo[:]).then_inc(q_done, 1)

            def project_k(b):
                three_terms(ps_work[0][:], wqkv_hi[:, 1, :], wqkv_lo[:, 1, :], xn_hi[:], xn_lo[:]).then_inc(k_done, 1)

            def project_vk(b, side):
                pe.wait_ge(q_ready if side == 0 else k_ready, b.count(1, 1))
                for t in range(2):
                    toks = slice((2 * side + t) * P, (2 * side + t + 1) * P)
                    out = ps_work[1 - side][:, t * 2 * D:(t + 1) * 2 * D]
                    vk_hi, vk_lo = wqkv_hi[:, 2:0:-1, :], wqkv_lo[:, 2:0:-1, :]
                    mm(out, xn_hi[:, toks], vk_hi, start=True, stop=False)
                    mm(out, xn_hi[:, toks], vk_lo, start=False, stop=False)
                    ins = mm(out, xn_lo[:, toks], vk_hi, start=False, stop=True)
                ins.then_inc(vk_done, 1)

            def score(b, pair):
                if pair == 0:
                    pe.wait_ge(k_ready, b.count(1, 1))
                    pe.wait_ge(q_heads_dve, b.count(2, 2))
                    pe.wait_ge(q_heads_act, b.count(1, 1))
                if pair >= 2:
                    pe.wait_ge(scores_ready, b.count(NT, pair - 1))
                for side in range(2):
                    toks = slice((2 * pair + side) * CH, (2 * pair + side + 1) * CH)
                    ins = mm(ps_score[pair % 2][side * CH:(side + 1) * CH, :], k_feat[b.parity][:, toks],
                             q_exp[b.parity][:, :, toks], start=True, stop=True)
                ins.then_inc(scores_done, 1)

            def hidden(b, f):
                if f == 0:
                    pe.wait_ge(vk_ready, b.count(2, 2))
                    pe.wait_ge(w1_split, 1)
                if f >= 2:
                    pe.wait_ge(relu_ready, b.count(NF, f - 1))
                cols = slice(f * P, (f + 1) * P)
                three_terms(ps_work[f % 2][:], w1_hi[:, cols], w1_lo[:, cols], xn_hi[:], xn_lo[:]).then_inc(h_done, 1)

            def chunk(b, c):
                pair, side = c // 2, c % 2
                rows = slice(side * CH, (side + 1) * CH)
                cols = slice(pair * CH, (pair + 1) * CH)
                if c == 0:
                    pe.wait_ge(vk_ready, b.count(2, 2))
                if side == 0:
                    pe.wait_ge(scores_ready, b.count(NT, pair + 1))
                if c > 0:
                    pe.wait_ge(state_ready, b.count(NCH - 1, c))
                if c < NCH - 1:
                    mm(ps_state[:, 0:D], k_tok[b.parity][rows, pair, :],
                       v_slots(v_pad[b.parity][:])[rows, pair], start=(c == 0), stop=True,
                       skip_group_check=True).then_inc(state_done, 1)
                if c > 0:
                    mm(ps_o[side][:, cols], state[c % 2][:],
                       q_dec[b.parity][:, c * CH:(c + 1) * CH], start=True, stop=False)
                for s in range(HEADS_IN_GROUP):
                    for g in range(NG):
                        ins = mm(ps_o[side][g * GW:(g + 1) * GW, cols],
                                 v_pad[b.parity][rows, pair, g, s * GW:(s + 1) * GW],
                                 scores[rows, pair, g * HEADS_IN_GROUP + s, :],
                                 start=(c == 0 and s == 0), stop=(s == HEADS_IN_GROUP - 1))
                if c >= NCH - 2:
                    ins.then_inc(o_done, 1)

            def second_product(b, tiles):
                for f in tiles:
                    pe.wait_ge(hi_ready, b.count(NF, f + 1))
                    mm(ps_y[:], w2[:, f, :], sq_hi[:, f, :], start=(f == 0), stop=False)
                    pe.wait_ge(lo_ready, b.count(NF, f + 1))
                    mm(ps_y[:], w2[:, f, :], sq_lo[:, f, :], start=False, stop=False)

            def output_product(b):
                pe.wait_ge(o_ready, b.count(2, 2))
                mm(ps_y[:], wo[:], o_feat[:].rearrange("p t s c -> p (t s c)"), start=False,
                   stop=True).then_inc(y_done, 1)

            first = Batch(0, 0)
            pe.wait_ge(consts_in, 16)
            turn_xn(first)
            pe.wait_ge(rank_loaded, 16)
            mm(ps_y[0:RANK, 0:D], fb_in, v_in, start=True, stop=True).then_inc(fbv_done, 1)
            pe.wait_ge(wqkv_split, 1)
            project_q(first)
            project_k(first)
            pe.wait_ge(tern_ready, 1)
            for t in range(NF):
                ins = nc.tensor.transpose(ps_o[0][:, t * P:(t + 1) * P], fc_scaled[:, t, :], ident)
            ins.then_inc(weights_turned, 1)
            project_vk(first, 0)
            pe.wait_ge(fbv_gated, 1)
            mm(ps_o[1][:], fbv[:], u_in, start=True, stop=True).then_inc(low_rank_done, 1)
            project_vk(first, 1)
            pe.wait_ge(tern_ready, 2)
            for t in range(NF):
                ins = nc.tensor.transpose(ps_state[:, t * P:(t + 1) * P], proj_tern[:, t * P:(t + 1) * P], ident)
            ins.then_inc(weights_turned, 1)
            nc.tensor.transpose(ps_y[:, 0:D], wo_scaled[:], ident).then_inc(weights_turned, 1)

            def body(b, later):
                nxt, ahead = b.next(), b.next().next()
                score(b, 0)
                hidden(b, 0)
                score(b, 1)
                hidden(b, 1)
                pe.wait_ge(weights_copied, 3)
                chunk(b, 0)
                hidden(b, 2)
                chunk(b, 1)
                hidden(b, 3)
                if later > 0:
                    turn_xn(nxt, b)
                chunk(b, 2)
                score(b, 2)
                if later > 0:
                    project_q(nxt, b)
                chunk(b, 3)
                if later > 0:
                    project_k(nxt)
                chunk(b, 4)
                score(b, 3)
                if later > 0:
                    project_vk(nxt, 0)
                chunk(b, 5)
                if later > 0:
                    project_vk(nxt, 1)
                chunk(b, 6)
                second_product(b, range(0, 2))
                chunk(b, 7)
                second_product(b, range(2, NF))
                output_product(b)

            over_batches(pe, body)


def kernel(L0_attn_hidden_states, L0_attn_rel_pos, L0_attn_Wq, L0_attn_Wk, L0_attn_Wv, L0_attn_Wo,
           L0_ffn_fast_b, L0_ffn_w_fc, L0_ffn_w_proj, L0_ffn_u, L0_ffn_v, L0_ffn_gate):
    import concourse.bacc as bacc
    from concourse.bass_utils import run_bass_kernel_spmd

    x = np.asarray(L0_attn_hidden_states).reshape(TOK, D)
    w_fc = np.asarray(L0_ffn_w_fc).reshape(NF, P, D).transpose(1, 0, 2).reshape(P, NF * D)
    gate = np.broadcast_to(np.asarray(L0_ffn_gate).reshape(1, 1), (RANK, 1))
    arrays = {
        "x_tok": x,
        "x_feat": x.T,
        "qkv_weights": np.stack([np.asarray(w) for w in (L0_attn_Wq, L0_attn_Wk, L0_attn_Wv)], axis=1),
        "ffn_weights": np.concatenate([w_fc, np.asarray(L0_ffn_w_proj), np.asarray(L0_attn_Wo).T], axis=1),
        "rank_weights": np.concatenate([np.asarray(L0_ffn_fast_b).T, np.asarray(L0_ffn_u).T,
                                        np.asarray(L0_ffn_v), gate], axis=1),
        "const": constants(),
    }
    arrays = {name: np.ascontiguousarray(a) for name, a in arrays.items()}
    nc = bacc.Bacc("TRN2", target_bir_lowering=False, num_devices=1)
    args = [nc.dram_tensor(name, a.shape, mybir.dt.from_np(a.dtype), kind="ExternalInput").ap()
            for name, a in arrays.items()]
    out = nc.dram_tensor("out_feat", (D, TOK), F32, kind="ExternalOutput").ap()
    build(nc, *args, out)
    r = run_bass_kernel_spmd(nc, [arrays], core_ids=[0])
    got = np.asarray(r.results[0]["out_feat"])
    return np.ascontiguousarray(got.T).reshape(NB, SEQ, D)
```

```python
from contextlib import ExitStack

import numpy as np

import concourse.bass as bass
from concourse import mybir

F32 = mybir.dt.float32
F32R = mybir.dt.float32r
ALU = mybir.AluOpType
ACT = mybir.ActivationFunctionType

P = 128
D = 128
H = 8
DK = D // H
SEQ = 512
NB = 8
TOK = NB * SEQ
CH = P
NT = SEQ // CH
HALF = H // 2
DMA_HEADS = 4
FF = 512
NF = FF // P
RANK = 16
EPS = 1e-5
MIN_SCALE = 1e-5
HEADS_IN_GROUP = 2
NG = H // HEADS_IN_GROUP
GW = HEADS_IN_GROUP * DK

C_IDENT = 0
C_QTAB = C_IDENT + P
C_VTAB = C_QTAB + SEQ
C_BLOCK = C_VTAB + NT * H
C_CAUSAL = C_BLOCK + P
C_ROWS = C_CAUSAL + CH
C_ALL = C_ROWS + H


def constants():
    gamma = 1.0 - 2.0 ** (-5.0 - np.arange(H, dtype=np.float64))
    place = np.arange(SEQ)
    c = np.zeros((P, C_ALL), np.float64)
    c[:, C_IDENT:C_IDENT + P] = np.eye(P)
    head = np.arange(P) // DK
    c[:, C_QTAB:C_QTAB + SEQ] = gamma[head][:, None] ** (place + 1) * DK ** -0.5
    inverse = gamma[None, :] ** -(place[:, None] + 1.0)
    c[:, C_VTAB:C_VTAB + NT * H] = inverse.reshape(NT, P, H).transpose(1, 0, 2).reshape(P, NT * H)
    c[:, C_BLOCK:C_BLOCK + P] = head[:, None] == head[None, :]
    c[:, C_CAUSAL:C_CAUSAL + CH] = np.arange(CH)[None, :] >= np.arange(P)[:, None]
    c[:, C_ROWS:C_ROWS + H] = head[:, None] == np.arange(H)[None, :]
    return c.astype(np.float32)


class Batch:

    def __init__(self, half, parity):
        self.half, self.parity = half, parity
        self.index = half * 2 + parity

    def next(self):
        return Batch(self.half, 1) if self.parity == 0 else Batch(self.half + 1, 0)

    def count(self, per_batch, k):
        return self.index * per_batch + k


def over_batches(engine, body):
    with engine.Fori(0, NB // 2 - 1) as half:
        for parity in range(2):
            body(Batch(half, parity), 2)
    body(Batch(NB // 2 - 1, 0), 1)
    body(Batch(NB // 2 - 1, 1), 0)


def build(nc, x_tok, x_feat, qkv_weights, ffn_weights, rank_weights, const, out_feat):
    with ExitStack() as ctx:
        def sb(name, shape, dt=F32):
            return ctx.enter_context(nc.sbuf_tensor(name, shape, dt))

        def pb(name, shape):
            return ctx.enter_context(nc.psum_tensor(name, shape, F32))

        def sem(name):
            return ctx.enter_context(nc.semaphore(name))

        cst = sb("cst", [P, C_ALL])
        ident = cst[:, C_IDENT:C_IDENT + P]
        q_table = cst[:, C_QTAB:C_QTAB + SEQ]
        v_table = cst[:, C_VTAB:C_VTAB + NT * H].rearrange("p (t g s) -> p t g s", t=NT, s=HEADS_IN_GROUP)
        block_mask = cst[:, C_BLOCK:C_BLOCK + P]
        causal = cst[:, C_CAUSAL:C_CAUSAL + CH]
        head_rows = cst[:, C_ROWS:C_ROWS + H]
        wqkv = sb("wqkv", [P, 3, D])
        wqkv_hi = sb("wqkv_hi", [P, 3, D], F32R)
        wqkv_lo = sb("wqkv_lo", [P, 3, D], F32R)
        ffn_in = sb("ffn_in", [P, NF * D + FF + D])
        fc_in = ffn_in[:, 0:NF * D].rearrange("p (t d) -> p t d", d=D)
        proj_in = ffn_in[:, NF * D:NF * D + FF]
        wo_in = ffn_in[:, NF * D + FF:]
        wo_scaled = sb("wo_scaled", [P, D])
        wo_hi = sb("wo_hi", [P, D], F32R)
        wo_lo = sb("wo_lo", [P, D], F32R)
        fc_above = sb("fc_above", [P, NF, D])
        fc_below = sb("fc_below", [P, NF, D])
        fc_scaled = sb("fc_scaled", [P, NF, D])
        w1_hi = sb("w1_hi", [P, FF], F32R)
        w1_lo = sb("w1_lo", [P, FF], F32R)
        proj_above = sb("proj_above", [P, FF])
        proj_below = sb("proj_below", [P, FF])
        proj_tern = sb("proj_tern", [P, FF])
        w2 = sb("w2", [P, NF, D], F32R)
        absolute = sb("absolute", [P, FF])
        rank_in = sb("rank_in", [RANK, RANK + FF + D + 1])
        fb_in = rank_in[:, 0:RANK]
        u_in = rank_in[:, RANK:RANK + FF]
        v_in = rank_in[:, RANK + FF:RANK + FF + D]
        gate_in = rank_in[:, RANK + FF + D:]
        fbv = sb("fbv", [RANK, D])
        sums = sb("sums", [P, NF + 1])
        scale = sb("scale", [P, NF + 1])
        half_scale = sb("half_scale", [P, NF + 1])
        neg_half = sb("neg_half", [P, NF + 1])
        inv_scale2 = sb("inv_scale2", [P, 1])

        x_in = [sb(f"x_in{p}", [P, NT, D]) for p in range(2)]
        resid = sb("resid", [P, TOK])
        stats = sb("stats", [P, NT, 6])
        mean_var = sb("mean_var", [P, NT, 2])
        var_eps = sb("var_eps", [P, NT])
        std = sb("std", [P, NT])
        rstd0 = sb("rstd0", [P, NT])
        newton = sb("newton", [P, NT])
        newton2 = sb("newton2", [P, NT])
        rstd = sb("rstd", [P, NT])
        xn = sb("xn", [P, NT, D])
        xn_hi = sb("xn_hi", [P, SEQ], F32R)
        xn_lo = sb("xn_lo", [P, SEQ], F32R)
        q_dec = [sb(f"q_dec{p}", [P, SEQ]) for p in range(2)]
        q_parts = sb("q_parts", [P, 2, SEQ], F32R)
        q_exp = [sb(f"q_exp{p}", [P, H, 2, SEQ], F32R) for p in range(2)]
        k_hi = sb("k_hi", [P, SEQ], F32R)
        k_lo = sb("k_lo", [P, SEQ], F32R)
        k_tok = [sb(f"k_tok{p}", [P, NT, D]) for p in range(2)]
        v_pad = [sb(f"v_pad{p}", [P, NT, NG, HEADS_IN_GROUP * GW]) for p in range(2)]
        scores = [sb(f"scores{p}", [P, H, CH]) for p in range(2)]
        state = [sb(f"state{p}", [P, D]) for p in range(2)]
        o_hi = sb("o_hi", [P, SEQ], F32R)
        o_lo = sb("o_lo", [P, SEQ], F32R)
        square = sb("square", [P, NF, SEQ])
        sq_hi = sb("sq_hi", [P, NF, SEQ], F32R)
        sq_lo = sb("sq_lo", [P, NF, SEQ], F32R)

        ps_score = [pb(f"ps_score{p}", [P, HALF * CH]) for p in range(2)]
        ps_work = [pb(f"ps_work{p}", [P, SEQ]) for p in range(2)]
        ps_state = pb("ps_state", [P, SEQ])
        ps_o = pb("ps_o", [P, SEQ])
        ps_y = pb("ps_y", [P, SEQ])

        consts_in, x_loaded = sem("consts_in"), [sem(f"x_loaded{p}") for p in range(2)]
        wqkv_in, ffn_loaded, rank_loaded = sem("wqkv_in"), sem("ffn_loaded"), sem("rank_loaded")
        resid_loaded, out_stored = sem("resid_loaded"), sem("out_stored")
        zeroed, wqkv_rounded, wqkv_split = sem("zeroed"), sem("wqkv_rounded"), sem("wqkv_split")
        abs_summed, fc_step, proj_step = sem("abs_summed"), sem("fc_step"), sem("proj_step")
        fbv_done, fbv_gated, w1_done = sem("fbv_done"), sem("fbv_gated"), sem("w1_done")
        fc_ready, proj_ready = sem("fc_ready"), sem("proj_ready")
        inverse_ready, wo_ready = sem("inverse_ready"), sem("wo_ready")
        w1_rounded, w1_split, proj_turned = sem("w1_rounded"), sem("w1_split"), sem("proj_turned")
        w2_copied, wo_turned, wo_rounded, wo_split = sem("w2_copied"), sem("wo_turned"), sem("wo_rounded"), sem("wo_split")
        ln_step, var_ready, std_ready = sem("ln_step"), sem("var_ready"), sem("std_ready")
        rstd_ready, xn_ready = sem("rstd_ready"), sem("xn_ready")
        xt_done, xn_hi_ready, xn_lo_ready = sem("xt_done"), sem("xn_hi_ready"), sem("xn_lo_ready")
        q_done, k_done, vk_done = sem("q_done"), sem("k_done"), sem("vk_done")
        q_ready, vk_ready = sem("q_ready"), sem("vk_ready")
        q_hi_ready, q_lo_ready, q_spread = sem("q_hi_ready"), sem("q_lo_ready"), sem("q_spread")
        k_hi_ready, k_lo_ready = sem("k_hi_ready"), sem("k_lo_ready")
        scores_done, scores_ready = sem("scores_done"), sem("scores_ready")
        state_done, state_ready = sem("state_done"), sem("state_ready")
        o_done, o_hi_ready, o_lo_ready = sem("o_done"), sem("o_hi_ready"), sem("o_lo_ready")
        h_done, relu_ready, square_ready = sem("h_done"), sem("relu_ready"), sem("square_ready")
        hi_ready, lo_ready = sem("hi_ready"), sem("lo_ready")
        y_done, result_ready = sem("y_done"), sem("result_ready")

        x_rows = x_tok.rearrange("(n t p) d -> p n t d", t=NT, p=P)

        def v_slots(v):
            return v.rearrange("p t g (s e) -> p t g s e", e=DK)[:, :, :, 0:4:3, :]

        block = ctx.enter_context(nc.Block())

        ZEROED_Q0, ZEROED_Q1 = 4, 5
        DVE_ZEROES = 3

        @block.sync
        def _(sync):
            sync.dma_start(x_in[0][:], x_rows[:, 0]).then_inc(x_loaded[0], 16)
            sync.dma_start(ffn_in[:], ffn_weights).then_inc(ffn_loaded, 16)
            sync.dma_start(x_in[1][:], x_rows[:, 1]).then_inc(x_loaded[1], 16)
            sync.dma_start(resid[:], x_feat).then_inc(resid_loaded, 16)

            def load_x(b, into):
                sync.wait_ge(xn_ready, b.index - 1)
                src = x_tok[bass.ds(b.index * SEQ, SEQ), :].rearrange("(t p) d -> p t d", p=P)
                sync.dma_start(x_in[into][:], src).then_inc(x_loaded[into], 16)

            def store(b):
                sync.wait_ge(result_ready, b.count(1, 1))
                cols = bass.ds(b.index * SEQ, SEQ)
                sync.dma_start(out_feat[:, cols], resid[:, cols]).then_inc(out_stored, 16)

            def spread_q(b, heads=H):
                sync.wait_ge(q_lo_ready, b.count(1, 1))
                for h in range(heads):
                    rows = slice(h * DK, (h + 1) * DK)
                    sync.dma_start(q_exp[b.parity][rows, h].bitcast(F32), q_parts[rows].bitcast(F32)).then_inc(q_spread, 16)

            def body(b, loads, spreads):
                if loads:
                    load_x(b.next().next().next(), 1 - b.parity)
                if spreads:
                    spread_q(b.next())
                store(b)

            sync.wait_ge(zeroed, ZEROED_Q0)
            spread_q(Batch(0, 0), DMA_HEADS)
            load_x(Batch(1, 0), 0)
            sync.wait_ge(zeroed, ZEROED_Q1)
            with sync.Fori(0, 2) as half:
                for parity in range(2):
                    body(Batch(half, parity), True, True)
            for index in range(4, NB):
                body(Batch(index // 2, index % 2), index + 3 < NB, index + 1 < NB)
            sync.wait_ge(out_stored, 16 * NB)

        @block.gpsimd
        def _(pool):
            nc.gpsimd.memset(q_exp[0][:, DVE_ZEROES:].bitcast(F32), 0.0).then_inc(zeroed, 1)
            for p in range(2):
                nc.gpsimd.memset(v_pad[p][:], 0.0).then_inc(zeroed, 1)

            own = slice(NF, NF + 1)
            pool.wait_ge(abs_summed, NF + 1)
            nc.gpsimd.tensor_scalar(scale[:, own], sums[:, own], 1.0 / FF, MIN_SCALE, ALU.mult,
                                    ALU.max).then_inc(proj_step, 1)
            pool.wait_ge(proj_step, 1)
            nc.gpsimd.tensor_scalar(half_scale[:, own], scale[:, own], 0.5, None, ALU.mult)
            nc.gpsimd.tensor_scalar(neg_half[:, own], scale[:, own], -0.5, None, ALU.mult).then_inc(proj_step, 1)
            pool.wait_ge(proj_step, 2)
            nc.gpsimd.tensor_scalar(proj_above[:], proj_in, half_scale[:, own], None, ALU.is_gt)
            nc.gpsimd.tensor_scalar(proj_below[:], proj_in, neg_half[:, own], None, ALU.is_lt).then_inc(proj_step, 1)
            pool.wait_ge(proj_step, 3)
            nc.gpsimd.tensor_tensor(proj_tern[:], proj_above[:], proj_below[:], ALU.subtract).then_inc(proj_ready, 1)
            nc.gpsimd.memset(q_exp[1][:].bitcast(F32), 0.0).then_inc(zeroed, 1)

            def body(b, later):
                for f in range(NF):
                    pool.wait_ge(hi_ready, b.count(NF, f + 1))
                    nc.gpsimd.tensor_tensor(sq_lo[:, f, :], square[:, f, :], sq_hi[:, f, :].bitcast(F32),
                                            ALU.subtract).then_inc(lo_ready, 1)

            over_batches(pool, body)

        @block.scalar
        def _(act):
            act.dma_start(rank_in[:], rank_weights).then_inc(rank_loaded, 16)
            act.dma_start(wqkv[:], qkv_weights).then_inc(wqkv_in, 16)
            act.dma_start(cst[:], const).then_inc(consts_in, 16)

            def root(b):
                act.wait_ge(var_ready, b.count(1, 1))
                nc.scalar.activation(std[:], var_eps[:], ACT.Sqrt).then_inc(std_ready, 1)

            def round_xn(b):
                act.wait_ge(xt_done, b.count(1, 1))
                nc.scalar.activation(xn_hi[:], ps_work[0][:], ACT.Copy).then_inc(xn_hi_ready, 1)

            def high_q(b):
                act.wait_ge(q_ready, b.count(1, 1))
                nc.scalar.activation(q_parts[:, 0, :], q_dec[b.parity][:], ACT.Copy).then_inc(q_hi_ready, 1)

            def high_k(b):
                act.wait_ge(k_done, b.count(1, 1))
                nc.scalar.activation(k_hi[:], ps_work[0][:], ACT.Copy).then_inc(k_hi_ready, 1)

            first = Batch(0, 0)
            root(first)
            act.wait_ge(ffn_loaded, 16)
            for t in range(NF):
                nc.scalar.activation(absolute[:, t * D:(t + 1) * D], fc_in[:, t, :], ACT.Abs,
                                     accum_out=sums[:, t:t + 1]).then_inc(abs_summed, 1)
            act.wait_ge(wqkv_in, 16)
            nc.scalar.activation(wqkv_hi[:], wqkv[:], ACT.Copy).then_inc(wqkv_rounded, 1)
            act.wait_ge(abs_summed, NF)
            nc.scalar.activation(absolute[:], proj_in, ACT.Abs,
                                 accum_out=sums[:, NF:NF + 1]).then_inc(abs_summed, 1)
            round_xn(first)
            high_q(first)
            high_k(first)
            act.wait_ge(w1_done, 1)
            nc.scalar.activation(w1_hi[:], ps_score[0][:], ACT.Copy).then_inc(w1_rounded, 1)
            act.wait_ge(zeroed, ZEROED_Q0)
            act.wait_ge(q_lo_ready, 1)
            for h in range(H - 2, H):
                for part in range(2):
                    ins = nc.scalar.activation(q_exp[0][:, h, part, :], q_parts[:, part, :].bitcast(F32), ACT.Copy,
                                               scale=head_rows[:, h:h + 1])
            ins.then_inc(q_spread, 32)
            root(first.next())
            act.wait_ge(proj_turned, 1)
            nc.scalar.activation(w2[:], ps_state[:].rearrange("p (t d) -> p t d", d=D),
                                 ACT.Copy).then_inc(w2_copied, 1)
            act.wait_ge(wo_turned, 1)
            nc.scalar.activation(wo_hi[:], ps_y[:, 0:D], ACT.Copy).then_inc(wo_rounded, 1)

            def take_relu(b, f):
                act.wait_ge(h_done, b.count(NF, f + 1))
                nc.scalar.activation(square[:, f, :], ps_work[f % 2][:], ACT.Relu).then_inc(relu_ready, 1)

            def high_square(b, f):
                act.wait_ge(square_ready, b.count(NF, f + 1))
                nc.scalar.activation(sq_hi[:, f, :], square[:, f, :], ACT.Copy).then_inc(hi_ready, 1)

            def take_square(b, f):
                act.wait_ge(relu_ready, b.count(NF, f + 1))
                nc.scalar.activation(square[:, f, :], square[:, f, :], ACT.Square).then_inc(square_ready, 1)

            def body(b, later):
                nxt, ahead = b.next(), b.next().next()
                take_relu(b, 0)
                take_relu(b, 1)
                take_square(b, 0)
                take_relu(b, 2)
                take_square(b, 1)
                take_relu(b, 3)
                if later > 1:
                    root(ahead)
                if later > 0:
                    round_xn(nxt)
                take_square(b, 2)
                take_square(b, 3)
                high_square(b, 0)
                high_square(b, 1)
                if later > 0:
                    high_q(nxt)
                high_square(b, 2)
                high_square(b, 3)
                if later > 0:
                    high_k(nxt)
                act.wait_ge(o_done, b.count(1, 1))
                nc.scalar.activation(o_hi[:], ps_o[:], ACT.Copy).then_inc(o_hi_ready, 1)

            over_batches(act, body)

        @block.vector
        def _(dve):
            LN_STEPS = 5

            def statistics(b):
                dve.wait_ge(x_loaded[b.parity], (b.half + 1) * 16)
                for t in range(NT):
                    ins = nc.vector.bn_stats(stats[:, t, :], x_in[b.parity][:, t, :])
                ins.then_inc(ln_step, 1)

            def variance(b):
                for t in range(NT):
                    ins = nc.vector.bn_aggr(mean_var[:, t, :], stats[:, t, :])
                ins.then_inc(ln_step, 1)
                dve.wait_ge(ln_step, b.count(LN_STEPS, 2))
                nc.vector.tensor_scalar(var_eps[:], mean_var[:, :, 1], EPS, None, ALU.add).then_inc(var_ready, 1)

            def inverse_root(b, step):
                if step == 0:
                    dve.wait_ge(std_ready, b.count(1, 1))
                    nc.vector.reciprocal(rstd0[:], std[:]).then_inc(ln_step, 1)
                elif step == 1:
                    dve.wait_ge(ln_step, b.count(LN_STEPS, 3))
                    nc.vector.tensor_tensor(newton[:], rstd0[:], var_eps[:], ALU.mult).then_inc(ln_step, 1)
                elif step == 2:
                    dve.wait_ge(ln_step, b.count(LN_STEPS, 4))
                    nc.vector.scalar_tensor_tensor(out=newton2[:], in0=newton[:], scalar=-0.5, in1=rstd0[:],
                                                   op0=ALU.mult, op1=ALU.mult).then_inc(ln_step, 1)
                else:
                    dve.wait_ge(ln_step, b.count(LN_STEPS, 5))
                    nc.vector.scalar_tensor_tensor(out=rstd[:], in0=newton2[:], scalar=1.5, in1=rstd0[:],
                                                   op0=ALU.add, op1=ALU.mult).then_inc(rstd_ready, 1)

            def normalise(b):
                dve.wait_ge(rstd_ready, b.count(1, 1))
                for t in range(NT):
                    ins = nc.vector.tensor_scalar(xn[:, t, :], x_in[b.parity][:, t, :], mean_var[:, t, 0:1],
                                                  rstd[:, t:t + 1], ALU.subtract, ALU.mult)
                ins.then_inc(xn_ready, 1)

            def low_xn(b):
                dve.wait_ge(xn_hi_ready, b.count(1, 1))
                nc.vector.tensor_tensor(xn_lo[:], ps_work[0][:], xn_hi[:].bitcast(F32),
                                        ALU.subtract).then_inc(xn_lo_ready, 1)

            def decay_q(b):
                dve.wait_ge(q_done, b.count(1, 1))
                nc.vector.tensor_tensor(q_dec[b.parity][:], ps_work[1][:], q_table,
                                        ALU.mult).then_inc(q_ready, 1)

            def low_q(b):
                dve.wait_ge(q_hi_ready, b.count(1, 1))
                nc.vector.tensor_tensor(q_parts[:, 1, :], q_dec[b.parity][:], q_parts[:, 0, :].bitcast(F32),
                                        ALU.subtract).then_inc(q_lo_ready, 1)

            def low_k(b):
                dve.wait_ge(k_hi_ready, b.count(1, 1))
                nc.vector.tensor_tensor(k_lo[:], ps_work[0][:], k_hi[:].bitcast(F32),
                                        ALU.subtract).then_inc(k_lo_ready, 1)

            def take_vk(b, side):
                dve.wait_ge(vk_done, b.count(2, side + 1))
                bank = ps_work[1 - side][:].rearrange("p (t w) -> p t w", t=2)
                tiles = slice(2 * side, 2 * side + 2)
                for t in range(2):
                    tile = 2 * side + t
                    nc.vector.tensor_tensor(
                        v_slots(v_pad[b.parity][:])[:, tile],
                        bank[:, t, 0:D].rearrange("p (g s e) -> p g s e", s=HEADS_IN_GROUP, e=DK),
                        v_table[:, tile].unsqueeze(3).broadcast_to([P, NG, HEADS_IN_GROUP, DK]), ALU.mult)
                nc.vector.tensor_copy(k_tok[b.parity][:, tiles, :], bank[:, :, D:2 * D]).then_inc(vk_ready, 1)

            def mask_scores(b, c, half):
                dve.wait_ge(scores_done, b.count(2 * NT, 2 * c + half + 1))
                nc.vector.tensor_tensor(
                    scores[c % 2][:, half * HALF:(half + 1) * HALF],
                    ps_score[half][:].rearrange("p (h i) -> p h i", h=HALF),
                    causal.unsqueeze(1).broadcast_to([P, HALF, CH]), ALU.mult).then_inc(scores_ready, 1)

            def take_state(b, c):
                dve.wait_ge(state_done, b.count(NT - 1, c))
                nc.vector.tensor_tensor(state[c % 2][:], ps_state[:, 0:D], block_mask,
                                        ALU.mult).then_inc(state_ready, 1)

            def low_output(b):
                dve.wait_ge(o_hi_ready, b.count(1, 1))
                nc.vector.tensor_tensor(o_lo[:], ps_o[:], o_hi[:].bitcast(F32),
                                        ALU.subtract).then_inc(o_lo_ready, 1)

            def finish(b):
                dve.wait_ge(y_done, b.count(1, 1))
                cols = bass.ds(b.index * SEQ, SEQ)
                nc.vector.scalar_tensor_tensor(out=resid[:, cols], in0=ps_y[:], scalar=scale[:, NF:NF + 1],
                                               in1=resid[:, cols], op0=ALU.mult,
                                               op1=ALU.add).then_inc(result_ready, 1)

            first = Batch(0, 0)
            nc.vector.memset(q_exp[0][:, 0:DVE_ZEROES].bitcast(F32), 0.0).then_inc(zeroed, 1)
            statistics(first)
            dve.wait_ge(fbv_done, 1)
            nc.vector.tensor_scalar(fbv[:], ps_y[0:RANK, 0:D], gate_in, None, ALU.mult).then_inc(fbv_gated, 1)
            dve.wait_ge(ln_step, 1)
            variance(first)
            for step in range(4):
                inverse_root(first, step)
            normalise(first)
            dve.wait_ge(abs_summed, NF)
            nc.vector.tensor_scalar(scale[:, 0:NF], sums[:, 0:NF], 1.0 / D, MIN_SCALE, ALU.mult,
                                    ALU.max).then_inc(fc_step, 1)
            dve.wait_ge(fc_step, 1)
            nc.vector.tensor_scalar(half_scale[:, 0:NF], scale[:, 0:NF], 0.5, None, ALU.mult)
            nc.vector.tensor_scalar(neg_half[:, 0:NF], scale[:, 0:NF], -0.5, None, ALU.mult).then_inc(fc_step, 1)
            dve.wait_ge(wqkv_rounded, 1)
            nc.vector.tensor_tensor(wqkv_lo[:], wqkv[:], wqkv_hi[:].bitcast(F32),
                                    ALU.subtract).then_inc(wqkv_split, 1)
            dve.wait_ge(fc_step, 2)

            def ternary_fc(t):
                nc.vector.tensor_scalar(fc_above[:, t, :], fc_in[:, t, :], half_scale[:, t:t + 1],
                                        scale[:, t:t + 1], ALU.is_gt, ALU.mult)
                return nc.vector.tensor_scalar(fc_below[:, t, :], fc_in[:, t, :], neg_half[:, t:t + 1],
                                               scale[:, t:t + 1], ALU.is_lt, ALU.mult)

            ternary_fc(0)
            low_xn(first)
            ternary_fc(1)
            ternary_fc(2)
            ternary_fc(3).then_inc(fc_step, 1)
            dve.wait_ge(proj_step, 1)
            nc.vector.reciprocal(inv_scale2[:], scale[:, NF:]).then_inc(inverse_ready, 1)
            dve.wait_ge(inverse_ready, 1)
            nc.vector.tensor_scalar(wo_scaled[:], wo_in, inv_scale2[:], None, ALU.mult).then_inc(wo_ready, 1)
            dve.wait_ge(consts_in, 16)
            decay_q(first)
            dve.wait_ge(fc_step, 3)
            nc.vector.tensor_tensor(fc_scaled[:], fc_above[:], fc_below[:], ALU.subtract).then_inc(fc_ready, 1)
            low_q(first)
            low_k(first)
            dve.wait_ge(zeroed, ZEROED_Q0)
            dve.wait_ge(q_lo_ready, 1)
            for h in range(DMA_HEADS, H - 2):
                for part in range(2):
                    ins = nc.vector.tensor_scalar(q_exp[0][:, h, part, :], q_parts[:, part, :].bitcast(F32),
                                                  head_rows[:, h:h + 1], None, ALU.mult)
            ins.then_inc(q_spread, 32)
            take_vk(first, 0)
            dve.wait_ge(w1_rounded, 1)
            nc.vector.tensor_tensor(w1_lo[:], ps_score[0][:], w1_hi[:].bitcast(F32),
                                    ALU.subtract).then_inc(w1_split, 1)
            take_vk(first, 1)
            statistics(first.next())
            dve.wait_ge(ln_step, first.next().count(LN_STEPS, 1))
            variance(first.next())
            for step in range(4):
                inverse_root(first.next(), step)
            normalise(first.next())
            dve.wait_ge(wo_rounded, 1)
            nc.vector.tensor_tensor(wo_lo[:], ps_y[:, 0:D], wo_hi[:].bitcast(F32),
                                    ALU.subtract).then_inc(wo_split, 1)
            dve.wait_ge(resid_loaded, 16)

            def body(b, later):
                nxt, ahead = b.next(), b.next().next()

                if later > 1:
                    statistics(ahead)
                    dve.wait_ge(ln_step, ahead.count(LN_STEPS, 1))
                mask_scores(b, 0, 0)
                if later > 1:
                    variance(ahead)
                mask_scores(b, 0, 1)
                mask_scores(b, 1, 0)
                take_state(b, 1)
                if later > 0:
                    low_xn(nxt)
                mask_scores(b, 1, 1)
                if later > 1:
                    inverse_root(ahead, 0)
                mask_scores(b, 2, 0)
                if later > 0:
                    decay_q(nxt)
                take_state(b, 2)
                if later > 0:
                    low_q(nxt)
                mask_scores(b, 2, 1)
                if later > 1:
                    inverse_root(ahead, 1)
                take_state(b, 3)
                mask_scores(b, 3, 0)
                if later > 1:
                    inverse_root(ahead, 2)
                mask_scores(b, 3, 1)
                if later > 1:
                    inverse_root(ahead, 3)
                if later > 0:
                    low_k(nxt)
                    take_vk(nxt, 0)
                low_output(b)
                if later > 0:
                    take_vk(nxt, 1)
                if later > 1:
                    normalise(ahead)
                finish(b)

            over_batches(dve, body)

        @block.tensor
        def _(pe):
            mm = nc.tensor.matmul

            def turn_xn(b, after=None):
                pe.wait_ge(xn_ready, b.count(1, 1))
                if after is not None:
                    pe.wait_ge(relu_ready, after.count(NF, 3))
                for t in range(NT):
                    ins = nc.tensor.transpose(ps_work[0][:, t * P:(t + 1) * P], xn[:, t, :], ident)
                ins.then_inc(xt_done, 1)

            def three_terms(out, w_hi, w_lo, x_hi, x_lo):
                mm(out, w_hi, x_hi, start=True, stop=False)
                mm(out, w_hi, x_lo, start=False, stop=False)
                return mm(out, w_lo, x_hi, start=False, stop=True)

            def project_q(b, after=None):
                pe.wait_ge(xn_hi_ready, b.count(1, 1))
                pe.wait_ge(xn_lo_ready, b.count(1, 1))
                if after is not None:
                    pe.wait_ge(relu_ready, after.count(NF, 4))
                three_terms(ps_work[1][:], wqkv_hi[:, 0, :], wqkv_lo[:, 0, :], xn_hi[:], xn_lo[:]).then_inc(q_done, 1)

            def project_k(b):
                three_terms(ps_work[0][:], wqkv_hi[:, 1, :], wqkv_lo[:, 1, :], xn_hi[:], xn_lo[:]).then_inc(k_done, 1)

            def project_vk(b, side):
                pe.wait_ge(q_ready if side == 0 else k_lo_ready, b.count(1, 1))
                for t in range(2):
                    toks = slice((2 * side + t) * P, (2 * side + t + 1) * P)
                    out = ps_work[1 - side][:, t * 2 * D:(t + 1) * 2 * D]
                    vk_hi, vk_lo = wqkv_hi[:, 2:0:-1, :], wqkv_lo[:, 2:0:-1, :]
                    mm(out, xn_hi[:, toks], vk_hi, start=True, stop=False)
                    mm(out, xn_hi[:, toks], vk_lo, start=False, stop=False)
                    ins = mm(out, xn_lo[:, toks], vk_hi, start=False, stop=True)
                ins.then_inc(vk_done, 1)

            def score(b, c, half):
                if c == 0 and half == 0:
                    pe.wait_ge(k_lo_ready, b.count(1, 1))
                    pe.wait_ge(q_spread, b.count(16 * H, 16 * H))
                if c > 0:
                    pe.wait_ge(scores_ready, b.count(2 * NT, 2 * c + half - 1))
                toks = slice(c * CH, (c + 1) * CH)
                q_hi, q_lo = (q_exp[b.parity][:, half * HALF:(half + 1) * HALF, part, toks] for part in range(2))
                three_terms(ps_score[half][:], k_hi[:, toks], k_lo[:, toks], q_hi, q_lo).then_inc(scores_done, 1)

            def hidden(b, f):
                if f == 0:
                    pe.wait_ge(vk_ready, b.count(2, 2))
                    pe.wait_ge(w1_split, 1)
                if f >= 2:
                    pe.wait_ge(relu_ready, b.count(NF, f - 1))
                cols = slice(f * P, (f + 1) * P)
                three_terms(ps_work[f % 2][:], w1_hi[:, cols], w1_lo[:, cols], xn_hi[:], xn_lo[:]).then_inc(h_done, 1)

            def carry(b, c):
                if c > 0:
                    pe.wait_ge(state_ready, b.count(NT - 1, c))
                    mm(ps_o[:, c * CH:(c + 1) * CH], state[c % 2][:],
                       q_dec[b.parity][:, c * CH:(c + 1) * CH], start=True, stop=False)
                if c < NT - 1:
                    mm(ps_state[:, 0:D], k_tok[b.parity][:, c, :], v_slots(v_pad[b.parity][:])[:, c],
                       start=(c == 0), stop=True, skip_group_check=True).then_inc(state_done, 1)

            def own_values(b, c):
                pe.wait_ge(scores_ready, b.count(2 * NT, 2 * c + 2))
                for s in range(HEADS_IN_GROUP):
                    for g in range(NG):
                        ins = mm(ps_o[g * GW:(g + 1) * GW, c * CH:(c + 1) * CH],
                                 v_pad[b.parity][:, c, g, s * GW:(s + 1) * GW],
                                 scores[c % 2][:, g * HEADS_IN_GROUP + s, :],
                                 start=(c == 0 and s == 0), stop=(s == HEADS_IN_GROUP - 1))
                if c == NT - 1:
                    ins.then_inc(o_done, 1)

            def second_product(b, tiles):
                for f in tiles:
                    pe.wait_ge(hi_ready, b.count(NF, f + 1))
                    mm(ps_y[:], w2[:, f, :], sq_hi[:, f, :], start=(f == 0), stop=False)
                    pe.wait_ge(lo_ready, b.count(NF, f + 1))
                    mm(ps_y[:], w2[:, f, :], sq_lo[:, f, :], start=False, stop=False)

            def output_product(b):
                pe.wait_ge(o_lo_ready, b.count(1, 1))
                pe.wait_ge(wo_split, 1)
                mm(ps_y[:], wo_hi[:], o_hi[:], start=False, stop=False)
                mm(ps_y[:], wo_hi[:], o_lo[:], start=False, stop=False)
                mm(ps_y[:], wo_lo[:], o_hi[:], start=False, stop=True).then_inc(y_done, 1)

            first = Batch(0, 0)
            pe.wait_ge(rank_loaded, 16)
            mm(ps_y[0:RANK, 0:D], fb_in, v_in, start=True, stop=True).then_inc(fbv_done, 1)
            pe.wait_ge(fbv_gated, 1)
            mm(ps_score[0][:], fbv[:], u_in, start=True, stop=True)
            pe.wait_ge(consts_in, 16)
            turn_xn(first)
            pe.wait_ge(wqkv_split, 1)
            project_q(first)
            project_k(first)
            pe.wait_ge(fc_ready, 1)
            for t in range(NF):
                ins = mm(ps_score[0][:, t * P:(t + 1) * P], fc_scaled[:, t, :], ident, start=False, stop=True,
                         skip_group_check=True)
            ins.then_inc(w1_done, 1)
            project_vk(first, 0)
            project_vk(first, 1)
            pe.wait_ge(proj_ready, 1)
            for t in range(NF):
                ins = nc.tensor.transpose(ps_state[:, t * P:(t + 1) * P], proj_tern[:, t * P:(t + 1) * P], ident)
            ins.then_inc(proj_turned, 1)
            pe.wait_ge(wo_ready, 1)
            nc.tensor.transpose(ps_y[:, 0:D], wo_scaled[:], ident).then_inc(wo_turned, 1)

            def body(b, later):
                nxt, ahead = b.next(), b.next().next()
                hidden(b, 0)
                hidden(b, 1)
                score(b, 0, 0)
                score(b, 0, 1)
                hidden(b, 2)
                score(b, 1, 0)
                hidden(b, 3)
                if later > 0:
                    turn_xn(nxt, b)
                pe.wait_ge(w2_copied, 1)
                carry(b, 0)
                score(b, 1, 1)
                own_values(b, 0)
                score(b, 2, 0)
                if later > 0:
                    project_q(nxt, b)
                carry(b, 1)
                own_values(b, 1)
                score(b, 2, 1)
                carry(b, 2)
                score(b, 3, 0)
                if later > 0:
                    project_vk(nxt, 0)
                score(b, 3, 1)
                if later > 0:
                    project_k(nxt)
                own_values(b, 2)
                carry(b, 3)
                own_values(b, 3)
                if later > 0:
                    project_vk(nxt, 1)
                second_product(b, range(0, NF))
                output_product(b)

            over_batches(pe, body)


def kernel(L0_attn_hidden_states, L0_attn_rel_pos, L0_attn_Wq, L0_attn_Wk, L0_attn_Wv, L0_attn_Wo,
           L0_ffn_fast_b, L0_ffn_w_fc, L0_ffn_w_proj, L0_ffn_u, L0_ffn_v, L0_ffn_gate):
    import concourse.bacc as bacc
    from concourse.bass_utils import run_bass_kernel_spmd

    x = np.asarray(L0_attn_hidden_states).reshape(TOK, D)
    w_fc = np.asarray(L0_ffn_w_fc).reshape(NF, P, D).transpose(1, 0, 2).reshape(P, NF * D)
    gate = np.broadcast_to(np.asarray(L0_ffn_gate).reshape(1, 1), (RANK, 1))
    arrays = {
        "x_tok": x,
        "x_feat": x.T,
        "qkv_weights": np.stack([np.asarray(w) for w in (L0_attn_Wq, L0_attn_Wk, L0_attn_Wv)], axis=1),
        "ffn_weights": np.concatenate([w_fc, np.asarray(L0_ffn_w_proj), np.asarray(L0_attn_Wo).T], axis=1),
        "rank_weights": np.concatenate([np.asarray(L0_ffn_fast_b).T, np.asarray(L0_ffn_u).T,
                                        np.asarray(L0_ffn_v), gate], axis=1),
        "const": constants(),
    }
    arrays = {name: np.ascontiguousarray(a) for name, a in arrays.items()}
    nc = bacc.Bacc("TRN2", target_bir_lowering=False, num_devices=1)
    args = [nc.dram_tensor(name, a.shape, mybir.dt.from_np(a.dtype), kind="ExternalInput").ap()
            for name, a in arrays.items()]
    out = nc.dram_tensor("out_feat", (D, TOK), F32, kind="ExternalOutput").ap()
    build(nc, *args, out)
    r = run_bass_kernel_spmd(nc, [arrays], core_ids=[0])
    got = np.asarray(r.results[0]["out_feat"])
    return np.ascontiguousarray(got.T).reshape(NB, SEQ, D)
```
